# Optimizing a Trainium2 kernel written in Bass

```python
import numpy as np
import jax
import jax.numpy as jnp

def _softmax(x, axis=-1):
    return jax.nn.softmax(x, axis=axis)

def _gelu(x):
    return jax.nn.gelu(x, approximate=True)

def _silu(x):
    return jax.nn.silu(x)

def _sigmoid(x):
    return jax.nn.sigmoid(x)

def _layernorm(x, axis=-1, eps=1e-05):
    m = jnp.mean(x, axis=axis, keepdims=True)
    v = jnp.var(x, axis=axis, keepdims=True)
    return (x - m) / jnp.sqrt(v + eps)

def _scatter_add(tgt, idx, src, axis=0):
    return tgt.at[idx].add(src)

def _segment_sum(src, seg, n):
    return jax.ops.segment_sum(src, seg, n)
kernel_name = 'mk_audio_tower_d2_tok_audfeat256_r4_5712c7'

def setup_inputs(seed: int=0):
    np.random.seed(seed)
    _w = jnp.asarray

    def _rec_inputs():
        import jax
        import jax.numpy as jnp
        _rk = jax.random.key(seed)
        x = 7.22013e-05 + 1.00017 * jax.random.normal(jax.random.fold_in(_rk, 1), (16, 750, 64), jnp.float32)
        return x
    x = _rec_inputs()

    def _L0_tok_setup():
        import jax, jax.numpy as jnp
        import numpy as np
        B, T, D = (8, 1024, 64)
        N_RECUR = 2
        TW = 15
        STRIDE = 2
        key = jax.random.key(seed)
        ks = jax.random.split(key, 8)
        glorot = (2.0 / (D + D)) ** 0.5
        X = jax.random.normal(ks[0], (B, T, D), dtype=jnp.float32)
        W_in = jax.random.normal(ks[1], (N_RECUR, D, D), dtype=jnp.float32) * glorot
        b_in = jax.random.normal(ks[2], (N_RECUR, D), dtype=jnp.float32) * 0.05
        W_out = jax.random.normal(ks[3], (N_RECUR, D, D), dtype=jnp.float32) * glorot
        b_out = jax.random.normal(ks[4], (N_RECUR, D), dtype=jnp.float32) * 0.05
        core_diag = jnp.ones((D,), dtype=jnp.float32)
        conv_filter = jax.random.normal(ks[5], (TW,), dtype=jnp.float32) * (2.0 / (TW + 1)) ** 0.5
        return {'X': X, 'W_in': W_in, 'b_in': b_in, 'W_out': W_out, 'b_out': b_out, 'core_diag': core_diag, 'conv_filter': conv_filter, 'stride': STRIDE}
    _L0_tok_all = _L0_tok_setup()
    _L0_tok_in = {k: v for k, v in _L0_tok_all.items() if k in ('W_in', 'b_in', 'W_out', 'b_out', 'core_diag', 'conv_filter')}
    del _L0_tok_all

    def _L0_attn_setup():
        import jax, jax.numpy as jnp
        import numpy as np
        GAMMA = 0.96875
        SCALE_BASE = 512.0

        def xpos_rope(x, downscale=False):
            B, S, D = x.shape
            half = D // 2
            inv_freq = 1.0 / 10000.0 ** (jnp.arange(0, D, 2, dtype=jnp.float32) / D)
            pos = jnp.arange(S, dtype=jnp.float32)
            ang = pos[:, None] * inv_freq[None, :]
            sin, cos = (jnp.sin(ang), jnp.cos(ang))
            base = (jnp.arange(0, D, 2, dtype=jnp.float32) + 0.4 * D) / (1.4 * D)
            scale = base[None, :] ** (pos[:, None] / SCALE_BASE)
            if downscale:
                scale = 1.0 / scale
            x1 = x[..., 0::2]
            x2 = x[..., 1::2]
            r1 = (x1 * cos - x2 * sin) * scale
            r2 = (x1 * sin + x2 * cos) * scale
            out = jnp.stack([r1, r2], axis=-1).reshape(B, S, D)
            return out

        def get_D(gamma, seq_len):
            n = jnp.arange(seq_len, dtype=jnp.float32)
            diff = n[:, None] - n[None, :]
            mask = diff >= 0
            D = jnp.where(mask, gamma ** jnp.where(mask, diff, 0.0), 0.0)
            return D

        def _reference_tuple_inner(x, W_Q, W_K, W_V):
            S = x.shape[1]
            D = get_D(GAMMA, S)
            Q = xpos_rope(x @ W_Q, downscale=False)
            K = xpos_rope(x @ W_K, downscale=True)
            V = x @ W_V
            ret = jnp.einsum('bnd,bmd->bnm', Q, K) * D[None, :, :]
            out = jnp.einsum('bnm,bmv->bnv', ret, V)
            return (out, ret)
        key = jax.random.key(seed)
        k1, k2, k3, k4 = jax.random.split(key, 4)
        B, S, d_model, d_k, d_v = (8, 1024, 64, 64, 64)
        x = jax.random.normal(k1, (B, S, d_model), dtype=jnp.float32)
        W_Q = jax.random.normal(k2, (d_model, d_k), dtype=jnp.float32) / d_model
        W_K = jax.random.normal(k3, (d_model, d_k), dtype=jnp.float32) / d_model
        W_V = jax.random.normal(k4, (d_model, d_v), dtype=jnp.float32) / d_model
        return {'x': x, 'W_Q': W_Q, 'W_K': W_K, 'W_V': W_V}
    _L0_attn_all = _L0_attn_setup()
    _L0_attn_in = {k: v for k, v in _L0_attn_all.items() if k in ('W_Q', 'W_K', 'W_V')}
    del _L0_attn_all

    def _L0_ffn_setup():
        import jax, jax.numpy as jnp
        import numpy as np
        DIM = 64
        HEADS = 8
        NUM_KEYS = 64
        NUM_KV = NUM_KEYS ** 2
        PK_TOPK = 16
        FINAL_TOPK = 16
        DIM_KEY = DIM // 2
        P = 2

        def _pk(x, Wq_pk, pk_keys):
            b, n, _ = x.shape
            q = (x @ Wq_pk).reshape(b, n, P, HEADS, DIM_KEY).transpose(2, 0, 1, 3, 4)
            sim = jnp.einsum('pbnhd,pkhd->pbnhk', q, pk_keys)
            scores, idx = jax.lax.top_k(sim, PK_TOPK)
            idx0 = idx[0]
            idx1 = idx[1] * NUM_KEYS
            index = (idx0[..., :, None] + idx1[..., None, :]).reshape(b, n, HEADS, PK_TOPK * PK_TOPK)
            score = (scores[0][..., :, None] + scores[1][..., None, :]).reshape(b, n, HEADS, PK_TOPK * PK_TOPK)
            final_scores, pk_idx = jax.lax.top_k(score, FINAL_TOPK)
            final_indices = jnp.take_along_axis(index, pk_idx, axis=-1)
            final_scores = jax.nn.softmax(final_scores, axis=-1)
            return (final_scores, final_indices)
        key = jax.random.key(seed)
        ks = jax.random.split(key, 7)
        b, n = (2, 256)
        std = 0.02
        x = jax.random.normal(ks[0], (b, n, DIM), dtype=jnp.float32)
        Wq_pk = jax.random.normal(ks[1], (DIM, P * HEADS * DIM_KEY), dtype=jnp.float32) * std
        pk_keys = jax.random.normal(ks[2], (P, NUM_KEYS, HEADS, DIM_KEY), dtype=jnp.float32) * std
        Wq = jax.random.normal(ks[3], (DIM, HEADS * DIM), dtype=jnp.float32) * std
        keys_table = jax.random.normal(ks[4], (NUM_KV * HEADS, DIM), dtype=jnp.float32) * std
        values_table = jax.random.normal(ks[5], (NUM_KV * HEADS, DIM), dtype=jnp.float32) * std
        Wo = jax.random.normal(ks[6], (DIM * HEADS, DIM), dtype=jnp.float32) * std
        return {'x': x, 'Wq_pk': Wq_pk, 'pk_keys': pk_keys, 'Wq': Wq, 'keys_table': keys_table, 'values_table': values_table, 'Wo': Wo}
    _L0_ffn_all = _L0_ffn_setup()
    _L0_ffn_in = {k: v for k, v in _L0_ffn_all.items() if k in ('Wq_pk', 'pk_keys', 'Wq', 'keys_table', 'values_table', 'Wo')}
    del _L0_ffn_all

    def _L1_attn_setup():
        import jax, jax.numpy as jnp
        import numpy as np
        D = 64
        L = 2
        B, S = (8, 1024)
        LR = 0.001
        WD = 0.01
        MAX_ALR = 0.1
        EPS = 1e-08

        def _lmm(Ws, bs, x):
            for i in range(L):
                x = x + jax.nn.silu(x @ Ws[i] + bs[i])
            return x

        def _reference_tuple_inner(x, Wk, Wq, Wv, Wlr, blr, Ws, bs):
            keys = x @ Wk
            queries = x @ Wq
            values = x @ Wv
            alr = (jax.nn.sigmoid(x @ Wlr + blr) * MAX_ALR).reshape(-1)

            def loss_fn(params):
                Ws_, bs_ = params
                preds = _lmm(Ws_, bs_, keys).reshape(-1, D)
                tgt = values.reshape(-1, D)
                per_tok = jnp.mean((preds - tgt) ** 2, axis=-1)
                return jnp.sum(per_tok * alr)
            gWs, gbs = jax.grad(loss_fn)((Ws, bs))

            def adamw_step(p, g):
                return p * (1.0 - LR * WD) - LR * g / (jnp.sqrt(g * g) + EPS)
            nWs = adamw_step(Ws, gWs)
            nbs = adamw_step(bs, gbs)
            retrieved = _lmm(nWs, nbs, queries)
            return (retrieved, -gWs, -gbs)
        key = jax.random.key(seed)
        ks = jax.random.split(key, 9)
        scale = 0.05
        return {'x': jax.random.normal(ks[0], (B, S, D), dtype=jnp.float32), 'Wk': jax.random.normal(ks[1], (D, D), dtype=jnp.float32) * scale, 'Wq': jax.random.normal(ks[2], (D, D), dtype=jnp.float32) * scale, 'Wv': jax.random.normal(ks[3], (D, D), dtype=jnp.float32) * scale, 'Wlr': jax.random.normal(ks[4], (D, 1), dtype=jnp.float32) * scale, 'blr': jnp.zeros((1,), dtype=jnp.float32), 'Ws': jax.random.normal(ks[5], (L, D, D), dtype=jnp.float32) * scale, 'bs': jnp.zeros((L, D), dtype=jnp.float32)}
    _L1_attn_all = _L1_attn_setup()
    _L1_attn_in = {k: v for k, v in _L1_attn_all.items() if k in ('Wk', 'Wq', 'Wv', 'Wlr', 'blr', 'Ws', 'bs')}
    del _L1_attn_all

    def _L1_ffn_setup():
        import jax, jax.numpy as jnp
        import numpy as np
        C = 64
        HID = 256
        E = 8
        TEMP = 1.0
        key = jax.random.key(seed)
        ks = jax.random.split(key, 7)
        x = jax.random.normal(ks[0], (8, 4096, C), dtype=jnp.float32)
        W1 = jax.random.normal(ks[1], (C, HID), dtype=jnp.float32) * 0.02
        b1 = jnp.zeros((HID,), dtype=jnp.float32)
        Wg = jax.random.normal(ks[2], (HID, E), dtype=jnp.float32) * 0.02
        bg = jnp.zeros((E,), dtype=jnp.float32)
        Wd = jax.random.normal(ks[3], (E, HID, C), dtype=jnp.float32) * 0.02
        bd = jnp.zeros((E, C), dtype=jnp.float32)
        return {'x': x, 'W1': W1, 'b1': b1, 'Wg': Wg, 'bg': bg, 'Wd': Wd, 'bd': bd}
    _L1_ffn_all = _L1_ffn_setup()
    _L1_ffn_in = {k: v for k, v in _L1_ffn_all.items() if k in ('W1', 'b1', 'Wg', 'bg', 'Wd', 'bd')}
    del _L1_ffn_all
    return {'x': x, 'L0_tok_W_in': _L0_tok_in['W_in'], 'L0_tok_b_in': _L0_tok_in['b_in'], 'L0_tok_W_out': _L0_tok_in['W_out'], 'L0_tok_b_out': _L0_tok_in['b_out'], 'L0_tok_core_diag': _L0_tok_in['core_diag'], 'L0_tok_conv_filter': _L0_tok_in['conv_filter'], 'L0_attn_W_Q': _L0_attn_in['W_Q'], 'L0_attn_W_K': _L0_attn_in['W_K'], 'L0_attn_W_V': _L0_attn_in['W_V'], 'L0_ffn_Wq_pk': _L0_ffn_in['Wq_pk'], 'L0_ffn_pk_keys': _L0_ffn_in['pk_keys'], 'L0_ffn_Wq': _L0_ffn_in['Wq'], 'L0_ffn_keys_table': _L0_ffn_in['keys_table'], 'L0_ffn_values_table': _L0_ffn_in['values_table'], 'L0_ffn_Wo': _L0_ffn_in['Wo'], 'L1_attn_Wk': _L1_attn_in['Wk'], 'L1_attn_Wq': _L1_attn_in['Wq'], 'L1_attn_Wv': _L1_attn_in['Wv'], 'L1_attn_Wlr': _L1_attn_in['Wlr'], 'L1_attn_blr': _L1_attn_in['blr'], 'L1_attn_Ws': _L1_attn_in['Ws'], 'L1_attn_bs': _L1_attn_in['bs'], 'L1_ffn_W1': _L1_ffn_in['W1'], 'L1_ffn_b1': _L1_ffn_in['b1'], 'L1_ffn_Wg': _L1_ffn_in['Wg'], 'L1_ffn_bg': _L1_ffn_in['bg'], 'L1_ffn_Wd': _L1_ffn_in['Wd'], 'L1_ffn_bd': _L1_ffn_in['bd']}

def reference(x, L0_tok_W_in, L0_tok_b_in, L0_tok_W_out, L0_tok_b_out, L0_tok_core_diag, L0_tok_conv_filter, L0_attn_W_Q, L0_attn_W_K, L0_attn_W_V, L0_ffn_Wq_pk, L0_ffn_pk_keys, L0_ffn_Wq, L0_ffn_keys_table, L0_ffn_values_table, L0_ffn_Wo, L1_attn_Wk, L1_attn_Wq, L1_attn_Wv, L1_attn_Wlr, L1_attn_blr, L1_attn_Ws, L1_attn_bs, L1_ffn_W1, L1_ffn_b1, L1_ffn_Wg, L1_ffn_bg, L1_ffn_Wd, L1_ffn_bd):
    import jax
    import jax.numpy as jnp

    def _L0_tok_ref(X, W_in, b_in, W_out, b_out, core_diag, conv_filter, stride):
        import jax, jax.numpy as jnp
        import numpy as np
        B, T, D = (8, 1024, 64)
        N_RECUR = 2
        TW = 15
        STRIDE = 2
        out = X
        for i in range(W_in.shape[0]):
            out = jnp.tanh(out @ W_in[i] + b_in[i])
        out = jnp.abs(core_diag)[None, None, :] * out * out
        n = W_out.shape[0]
        for i in range(n):
            out = jnp.tanh(out @ W_out[n - 1 - i] + b_out[n - 1 - i])
        tw = conv_filter.shape[0]
        pad = tw // 2
        out = jnp.pad(out, ((0, 0), (pad, pad), (0, 0)))
        d = out.shape[-1]
        kernel = jnp.broadcast_to(conv_filter[:, None, None], (tw, 1, d))
        out_pool = jax.lax.conv_general_dilated(out, kernel, window_strides=(stride,), padding='VALID', dimension_numbers=('NWC', 'WIO', 'NWC'), feature_group_count=d)
        return out_pool

    def _L0_attn_ref(x, W_Q, W_K, W_V):
        import jax, jax.numpy as jnp
        import numpy as np
        GAMMA = 0.96875
        SCALE_BASE = 512.0

        def xpos_rope(x, downscale=False):
            B, S, D = x.shape
            half = D // 2
            inv_freq = 1.0 / 10000.0 ** (jnp.arange(0, D, 2, dtype=jnp.float32) / D)
            pos = jnp.arange(S, dtype=jnp.float32)
            ang = pos[:, None] * inv_freq[None, :]
            sin, cos = (jnp.sin(ang), jnp.cos(ang))
            base = (jnp.arange(0, D, 2, dtype=jnp.float32) + 0.4 * D) / (1.4 * D)
            scale = base[None, :] ** (pos[:, None] / SCALE_BASE)
            if downscale:
                scale = 1.0 / scale
            x1 = x[..., 0::2]
            x2 = x[..., 1::2]
            r1 = (x1 * cos - x2 * sin) * scale
            r2 = (x1 * sin + x2 * cos) * scale
            out = jnp.stack([r1, r2], axis=-1).reshape(B, S, D)
            return out

        def get_D(gamma, seq_len):
            n = jnp.arange(seq_len, dtype=jnp.float32)
            diff = n[:, None] - n[None, :]
            mask = diff >= 0
            D = jnp.where(mask, gamma ** jnp.where(mask, diff, 0.0), 0.0)
            return D

        def _reference_tuple_inner(x, W_Q, W_K, W_V):
            S = x.shape[1]
            D = get_D(GAMMA, S)
            Q = xpos_rope(x @ W_Q, downscale=False)
            K = xpos_rope(x @ W_K, downscale=True)
            V = x @ W_V
            ret = jnp.einsum('bnd,bmd->bnm', Q, K) * D[None, :, :]
            out = jnp.einsum('bnm,bmv->bnv', ret, V)
            return (out, ret)
        return _reference_tuple_inner(x, W_Q, W_K, W_V)[0]

    def _L0_ffn_ref(x, Wq_pk, pk_keys, Wq, keys_table, values_table, Wo):
        import jax, jax.numpy as jnp
        import numpy as np
        DIM = 64
        HEADS = 8
        NUM_KEYS = 64
        NUM_KV = NUM_KEYS ** 2
        PK_TOPK = 16
        FINAL_TOPK = 16
        DIM_KEY = DIM // 2
        P = 2

        def _pk(x, Wq_pk, pk_keys):
            b, n, _ = x.shape
            q = (x @ Wq_pk).reshape(b, n, P, HEADS, DIM_KEY).transpose(2, 0, 1, 3, 4)
            sim = jnp.einsum('pbnhd,pkhd->pbnhk', q, pk_keys)
            scores, idx = jax.lax.top_k(sim, PK_TOPK)
            idx0 = idx[0]
            idx1 = idx[1] * NUM_KEYS
            index = (idx0[..., :, None] + idx1[..., None, :]).reshape(b, n, HEADS, PK_TOPK * PK_TOPK)
            score = (scores[0][..., :, None] + scores[1][..., None, :]).reshape(b, n, HEADS, PK_TOPK * PK_TOPK)
            final_scores, pk_idx = jax.lax.top_k(score, FINAL_TOPK)
            final_indices = jnp.take_along_axis(index, pk_idx, axis=-1)
            final_scores = jax.nn.softmax(final_scores, axis=-1)
            return (final_scores, final_indices)
        b, n, d = x.shape
        q = (x @ Wq).reshape(b, n, HEADS, DIM) * DIM ** (-0.5)
        kv_scores, indices = _pk(x, Wq_pk, pk_keys)
        offsets = jnp.arange(HEADS, dtype=indices.dtype) * NUM_KV
        ind = indices + offsets[None, None, :, None]
        k = jnp.einsum('bnhk,bnhkd->bnhd', kv_scores, keys_table[ind])
        v = jnp.einsum('bnhk,bnhkd->bnhd', kv_scores, values_table[ind])
        sim = jnp.einsum('bihd,bjhd->bhij', q, k)
        neg = -jnp.finfo(sim.dtype).max
        causal = jnp.tril(jnp.ones((n, n), dtype=bool))
        sim = jnp.where(causal, sim, neg)
        attn = jax.nn.softmax(sim, axis=-1)
        out = jnp.einsum('bhij,bjhd->bhid', attn, v)
        out = out.transpose(0, 2, 1, 3).reshape(b, n, HEADS * DIM)
        return out @ Wo

    def _L1_attn_ref(x, Wk, Wq, Wv, Wlr, blr, Ws, bs):
        import jax, jax.numpy as jnp
        import numpy as np
        D = 64
        L = 2
        B, S = (8, 1024)
        LR = 0.001
        WD = 0.01
        MAX_ALR = 0.1
        EPS = 1e-08

        def _lmm(Ws, bs, x):
            for i in range(L):
                x = x + jax.nn.silu(x @ Ws[i] + bs[i])
            return x

        def _reference_tuple_inner(x, Wk, Wq, Wv, Wlr, blr, Ws, bs):
            keys = x @ Wk
            queries = x @ Wq
            values = x @ Wv
            alr = (jax.nn.sigmoid(x @ Wlr + blr) * MAX_ALR).reshape(-1)

            def loss_fn(params):
                Ws_, bs_ = params
                preds = _lmm(Ws_, bs_, keys).reshape(-1, D)
                tgt = values.reshape(-1, D)
                per_tok = jnp.mean((preds - tgt) ** 2, axis=-1)
                return jnp.sum(per_tok * alr)
            gWs, gbs = jax.grad(loss_fn)((Ws, bs))

            def adamw_step(p, g):
                return p * (1.0 - LR * WD) - LR * g / (jnp.sqrt(g * g) + EPS)
            nWs = adamw_step(Ws, gWs)
            nbs = adamw_step(bs, gbs)
            retrieved = _lmm(nWs, nbs, queries)
            return (retrieved, -gWs, -gbs)
        return _reference_tuple_inner(x, Wk, Wq, Wv, Wlr, blr, Ws, bs)[0]

    def _L1_ffn_ref(x, W1, b1, Wg, bg, Wd, bd):
        import jax, jax.numpy as jnp
        import numpy as np
        C = 64
        HID = 256
        E = 8
        TEMP = 1.0
        orig_shape = x.shape
        xf = x.reshape(-1, orig_shape[-1])
        H = jax.nn.gelu(xf @ W1 + b1, approximate=False)
        probs = jax.nn.softmax((H @ Wg + bg) / TEMP, axis=-1)
        assign = jnp.argmax(probs, axis=-1)
        out = jnp.zeros_like(xf)
        for e in range(Wd.shape[0]):
            y = H @ Wd[e] + bd[e]
            sel = (assign == e)[:, None]
            out = out + jnp.where(sel, probs[:, e:e + 1] * y, 0.0)
        return out.reshape(orig_shape)
    h = _L0_tok_ref(x, L0_tok_W_in, L0_tok_b_in, L0_tok_W_out, L0_tok_b_out, L0_tok_core_diag, L0_tok_conv_filter, 2)
    h = h + _L0_attn_ref(_layernorm(h, axis=-1), L0_attn_W_Q, L0_attn_W_K, L0_attn_W_V)
    h = h + _L0_ffn_ref(_layernorm(h, axis=-1), L0_ffn_Wq_pk, L0_ffn_pk_keys, L0_ffn_Wq, L0_ffn_keys_table, L0_ffn_values_table, L0_ffn_Wo)
    h = h + _L1_attn_ref(_layernorm(h, axis=-1), L1_attn_Wk, L1_attn_Wq, L1_attn_Wv, L1_attn_Wlr, L1_attn_blr, L1_attn_Ws, L1_attn_bs)
    h = h + _L1_ffn_ref(_layernorm(h, axis=-1), L1_ffn_W1, L1_ffn_b1, L1_ffn_Wg, L1_ffn_bg, L1_ffn_Wd, L1_ffn_bd)
    return h

_drawn_inputs = setup_inputs


def setup_inputs(seed=0):
    import zlib

    import numpy as np

    out = dict(_drawn_inputs(seed))
    spreads = {'L0_tok_core_diag': (1.0, 0.2),
     'L1_attn_bs': (0.0, 0.1),
     'L1_ffn_b1': (0.0, 0.451),
     'L1_ffn_bg': (0.0, 0.1),
     'L1_ffn_bd': (0.0, 0.34)}
    factors = {'L0_ffn_Wq_pk': 8.0,
     'L0_ffn_pk_keys': 8.0,
     'L0_ffn_Wq': 23.623,
     'L0_ffn_keys_table': 28.425,
     'L0_ffn_values_table': 8.0,
     'L0_ffn_Wo': 8.0,
     'L1_attn_Wk': 32.155,
     'L1_attn_Wv': 22.928,
     'L1_attn_Wlr': 64.0,
     'L1_ffn_W1': 3.235,
     'L1_ffn_Wg': 3.423,
     'L1_ffn_Wd': 8.0}
    for name, (base, spread) in spreads.items():
        noise = np.random.default_rng([zlib.crc32(name.encode()), seed]).standard_normal(out[name].shape)
        drawn = base * np.exp(spread * noise) if base else spread * noise
        out[name] = jnp.asarray(drawn.astype(out[name].dtype))
    for name, factor in factors.items():
        out[name] = (out[name] * factor).astype(out[name].dtype)
    return out
```

```python
from contextlib import ExitStack

import numpy as np

import concourse.bass as bass
from concourse import mybir

F32 = mybir.dt.float32
U32 = mybir.dt.uint32
ALU = mybir.AluOpType
ACT = mybir.ActivationFunctionType
AX_X = mybir.AxisListType.X

B, S_IN, D = 16, 750, 64
TAPS, STRIDE = 15, 2
PAD = TAPS // 2
S = (S_IN + 2 * PAD - TAPS) // STRIDE + 1
P = 125
NT = S // P
HALF = S_IN // 2
H, K, SUB = 8, 16, 64
SLOTS = H * K
NKV = SUB * SUB
RUNS = [(a, K // (a + 1)) for a in range(K // 2)]
TAIL_AT = sum(n for _, n in RUNS)
CAND = TAIL_AT + K - K // 2
OFFS = [sum(n for _, n in RUNS[:i]) for i in range(len(RUNS))]
HH = 4
GROUPS, PER = 5, 25
HID, E = 256, 8
EPS = 1e-5
LOWEST = -3.0e38
LR, WD, GEPS = 1e-3, 1e-2, 1e-8
ALR_SCALE = 0.1 * 2.0 / D


class Alone:

    def __init__(self, engine, passed):
        self.engine, self.passed = engine, passed

    def wait_ge(self, semaphore, value):
        self.engine.wait_ge(semaphore, value)
        if not isinstance(value, int):
            self.engine.sem_inc(self.passed, 1)


def tower(nc, xT, w_in, b_in, w_out, b_out, core, taps, w_rope, w_v, pk_q, pk_keys, w_q, kv_table,
          w_o, m_k, m_q, m_v, m_lr, m_blr, m_params, m_b, m_w1T, f_w1, f_b1, f_wg, f_bg, f_wd,
          f_bd, c_rope, c_decay, c_mask, c_ident, c_iota, c_headoff, c_headmask, out):
    with ExitStack() as ctx:
        def sb(name, shape, dt=F32):
            return ctx.enter_context(nc.sbuf_tensor(name, shape, dt))

        def bank(name, n=1):
            return ctx.enter_context(nc.psum_tensor(name, [128, n, 512], F32))

        def sem(name):
            return ctx.enter_context(nc.semaphore(name))

        ident = sb("ident", [128, 128])
        rope_t = sb("rope_t", [D, 2, 2, S])
        decay = sb("decay", [P, S])
        mask = sb("mask", [P, 2, S])
        iota = sb("iota", [P, CAND])
        headoff = sb("headoff", [P, H, K])
        headmask = sb("headmask", [128, H])
        win_s = sb("win_s", [D, 2, D])
        wout_s = sb("wout_s", [D, 2, D])
        bias_s = sb("bias_s", [D, 4])
        core_s = sb("core_s", [D, 2])
        taps_s = sb("taps_s", [D, TAPS])
        tapdiag = sb("tapdiag", [D, TAPS, D])
        wrope_s = sb("wrope_s", [D, 4, D])
        wv_s = sb("wv_s", [D, D])
        simw = sb("simw", [D, 2 * H * SUB])
        wq_s = sb("wq_s", [D, H, D])
        wo_s = sb("wo_s", [128, H, D])
        mk_s = sb("mk_s", [D, D])
        mq_s = sb("mq_s", [D, D])
        mv_s = sb("mv_s", [D, D])
        mlr_s = sb("mlr_s", [D, 1])
        mlrb = sb("mlrb", [D, D])
        mblr_s = sb("mblr_s", [D, 1])
        params = sb("params", [D + 1, 2, D])
        mb_s = sb("mb_s", [D, 2])
        w1T_s = sb("w1T_s", [D, D])
        fw1_s = sb("fw1_s", [D, HID])
        fb1_s = sb("fb1_s", [128, HID // 128])
        fwg_s = sb("fwg_s", [128, HID // 128, E])
        fbg_s = sb("fbg_s", [1, E])
        fwd_s = sb("fwd_s", [128, HID // 128, E * D])
        fbd_s = sb("fbd_s", [1, E * D])
        ones = sb("ones", [1, P])
        eps = sb("eps", [P, 1])
        h2_saved = nc.dram_tensor("h2_saved", (B, P, NT * D), F32).ap()
        n3T_kept = nc.dram_tensor("n3T_kept", (B, D, S), F32).ap()
        grads = sb("grads", [D + 1, 2 * D])
        x_in = sb("x_in", [D, S_IN])
        front = sb("front", [128, 4 * HALF])
        tok = front[0:D].rearrange("p (n c t) -> p n c t", n=2, c=2)
        mixed = sb("mixed", [D, S_IN + 2 * PAD])
        h0 = sb("h0", [P, NT, D])
        stats = sb("stats", [P, NT, 6])
        mv = sb("mv", [P, NT, 2])
        std = sb("std", [P, NT])
        rstd = sb("rstd", [P, NT])
        nrm = sb("nrm", [P, NT, D])
        nT = sb("nT", [D, S])
        shared = sb("shared", [128, 4 * S + NT * H * D])
        ret = shared[0:P, 0:NT * S].rearrange("p (j s) -> p j s", j=NT)
        qk = sb("qk", [D, 2, S])
        qk_b = shared[0:D, NT * S:(NT + 2) * S].rearrange("p (j s) -> p j s", j=2)
        v_s = sb("v_s", [P, NT, D])
        h1 = sb("h1", [P, NT, D])
        n2T = sb("n2T", [D, S])
        s16 = sb("s16", [P, 2 * H, K])
        i16 = sb("i16", [P, 2 * H, K], U32)
        i16f = sb("i16f", [P, 2 * H, K])
        rest = front[0:P, 0:2 * H * SUB].rearrange("p (g k) -> p g k", k=SUB)
        cand = sb("cand", [P, H, CAND])
        cidx = sb("cidx", [P, H, CAND])
        crest = front[0:P, 2 * H * SUB:2 * H * SUB + H * CAND].rearrange("p (h c) -> p h c", c=CAND)
        f16 = sb("f16", [P, H, K])
        pos = sb("pos", [P, H, K], U32)
        posf = sb("posf", [P, H, K])
        picks = sb("picks", [128, HH * K * CAND])
        pick = picks[0:P].rearrange("p (n c) -> p n c", c=CAND)
        idxf = sb("idxf", [P, H, K])
        esum = sb("esum", [P, 2, H])
        wgt = sb("wgt", [P, H, K])
        wT_next = sb("wT_next", [128, S])
        idx_next = sb("idx_next", [128, S], U32)
        idx_now = sb("idx_now", [128, S], U32)
        wbd = sb("wbd", [128, S, H])
        rows = sb("rows", [128, GROUPS * PER, 2 * D])
        kvT = sb("kvT", [128, H, S])
        h1_now = sb("h1_now", [P, NT, D])
        n2T_now = sb("n2T_now", [D, S])
        vo = shared[0:P, 4 * S:].rearrange("p (j d) -> p j d", j=NT)
        qT = sb("qT", [D, 2, S])
        prob2 = sb("prob2", [P, 2 * S])
        prob = [shared[0:P, 0:2 * S].rearrange("p (j s) -> p j s", j=2), prob2[:].rearrange("p (j s) -> p j s", j=2)]
        pT = shared[0:P, 2 * S:4 * S].rearrange("p (j s) -> p j s", j=2)
        mx = sb("mx", [P, 2, NT])
        zs = sb("zs", [P, 4, NT])

        def regions(h):
            p = prob[h % 2]
            return p[:, 0, 0:P], p[:, 0, P:S], p[:, 1, 0:S]

        h2 = sb("h2", [P, NT, D])
        x0 = sb("x0", [D + 1, S])
        x1 = sb("x1", [D + 1, S])
        x2 = sb("x2", [D, S])
        sg = picks[0:D, 0:3 * S].rearrange("p (j s) -> p j s", j=3)
        s_a = picks[0:D, 3 * S:5 * S].rearrange("p (j s) -> p j s", j=2)
        d_a = picks[0:D, 5 * S:7 * S].rearrange("p (j s) -> p j s", j=2)
        g2 = picks[0:D, 7 * S:8 * S]
        n3T = sb("n3T", [D, S])
        dz = sb("dz", [D, 2, S])
        xt = sb("xt", [P, 2, NT, D + 1])
        dzt = sb("dzt", [P, 2, NT, D])
        upd = sb("upd", [D + 1, 3, 2 * D])
        lmax = sb("lmax", [P, 3, NT])
        e8 = sb("e8", [P, NT, E])
        p8 = sb("p8", [P, NT, E])
        m8 = sb("m8", [P, NT, 8])
        mi8 = sb("mi8", [P, NT, 8], U32)
        mif = sb("mif", [P, NT])
        c8 = sb("c8", [P, NT, E])
        wy = rows[0:P, 8:12, :].rearrange("p a d -> p (a d)").rearrange("p (e d) -> p e d", e=E)
        pkq_s = rows[0:D // 2, 0:8, :].rearrange("p a d -> p (a d)").rearrange("p (g d) -> p g d", d=D)
        pkk_s = rows[0:D // 2, 8:16, :].rearrange("p a d -> p (a d)").rearrange("p (g d) -> p g d", d=SUB)
        ysum = sb("ysum", [P, D])

        work = bank("work", 2)
        sims = bank("sims", 2)
        gath = bank("gath", 2)
        turn = bank("turn")
        accu = bank("accu")

        names = """loaded fold_mm fold_done prep tapd x_in x_used tok_mm tok_act tok_sq conv h0_done
            ln_stats ln_var ln_std ln_inv ln_n nT_mm nT_done ml_stats ml_var ml_std ml_inv ml_n nTm_mm nTm_done qk_mm v_done rope_a rope_b rope_done ret_mm
            ret_done mix_mm h1_done sim_mm sim_read top_a top_b top_c top_d cand_a cand_b fin_a
            fin_b fin_c fin_d fin_e pos_f pick_a pick_b pick_c fdiff fexp fsum frec wgt_done
            tw_mm wT_done ti_done next_ready idx_taken wbd_done kept freed rows_mm kv_done
            vo_mm vo_done q_mm q_done s_mm s_masked s_max s_exp s_rec s_norm pT_mm pT_done o_mm
            h2_done h2_kept n3_kept x0_mm x0_done alr_done z_mm sig_done silu_a silu_b x_done dd_a d_done
            err_a g2_done dz2_done dx_mm g1_done dz_done t_mm t_done g_mm g_done
            upd_a upd_b upd_c upd_d upd_e upd_done out_ready out_sent n3_now h2_now saved sent
            h_mm h_act y_mm lg_mm lg_d lg_rec lg_max lg_exp lg_sum lg_p lg_top lg_i lg_if lg_oh lg_c wy wy_sum
            pe_waits act_waits dve_waits sp_waits pool_waits""".split()
        assert len(names) == len(set(names))
        s = {n: sem(n) for n in names}
        got = [sem(f"got{g}") for g in range(GROUPS)]

        loads = [(ident, c_ident), (rope_t, c_rope), (decay, c_decay), (mask, c_mask), (iota, c_iota),
                 (headoff, c_headoff), (headmask, c_headmask),
                 (win_s, w_in.rearrange("n i o -> i n o")), (wout_s, w_out.rearrange("n i o -> i n o")),
                 (bias_s[:, 0:2], b_in), (bias_s[:, 2:4], b_out),
                 (core_s[:, 0:1], core.rearrange("(d a) -> d a", a=1)),
                 (taps_s, taps.rearrange("(a t) -> a t", a=1).broadcast_to([D, TAPS])),
                 (wrope_s, w_rope), (wv_s, w_v), (pkq_s, pk_q), (pkk_s, pk_keys),
                 (wq_s, w_q.rearrange("i (h o) -> i h o", h=H)),
                 (wo_s[D:128], w_o.rearrange("(h d) o -> d h o", h=H)),
                 (mk_s, m_k), (mq_s, m_q), (mv_s, m_v), (mlr_s, m_lr),
                 (mblr_s, m_blr.rearrange("(a t) -> a t", a=1).broadcast_to([D, 1])),
                 (params, m_params), (mb_s, m_b), (w1T_s, m_w1T),
                 (fw1_s, f_w1), (fb1_s, f_b1),
                 (fwg_s, f_wg.rearrange("(c p) e -> p c e", p=128)),
                 (fbg_s, f_bg.rearrange("(a t) -> a t", a=1)),
                 (fwd_s, f_wd), (fbd_s, f_bd)]
        ALL_LOADED = 16 * len(loads)

        def tile(t):
            return slice(t * P, (t + 1) * P)

        hid = rows[:, 0:2 * NT, :].rearrange("p a d -> p (a d)")[:, 0:2 * S].rearrange("p (c t) -> p c t", c=2)
        PAIRS = [(0, 0, 0), (1, 0, P), (1, 1, 2 * P), (2, 0, 0), (2, 1, P), (2, 2, 2 * P)]

        block = ctx.enter_context(nc.Block())

        @block.sync
        def _(sp):
            def full(x):
                return x if isinstance(x, bass.AP) else x[:]

            sp = Alone(nc.sync, s["sp_waits"])

            def load_x(b):
                nc.sync.dma_start(x_in[:], xT[b]).then_inc(s["x_in"], 16)

            def keep_n3(b):
                sp.wait_ge(s["nTm_done"], b + 1)
                nc.sync.dma_start(n3T_kept[b], n3T[:]).then_inc(s["n3_kept"], 16)
                nc.sync.dma_start(h2_saved[b], h2[:].rearrange("p t d -> p (t d)")).then_inc(s["h2_kept"], 16)
                sp.wait_ge(s["n3_kept"], b * 16 + 16)
                sp.wait_ge(s["h2_kept"], b * 16 + 16)
                nc.sync.sem_inc(s["saved"], 1)

            for dst, src in loads:
                nc.sync.dma_start(full(dst), full(src)).then_inc(s["loaded"], 16)
            load_x(0)
            nc.sync.sem_inc(s["saved"], 1)
            nc.sync.sem_inc(s["sent"], 1)
            with nc.sync.Fori(0, B - 1) as b:
                sp.wait_ge(s["tok_mm"], b * 4 + 1)
                load_x(b + 1)
                keep_n3(b)
            keep_n3(B - 1)
            def load_saved(b):
                sp.wait_ge(s["x0_mm"], b + B)
                nc.sync.dma_start(n2T[:], n3T_kept[b]).then_inc(s["n3_now"], 16)
                sp.wait_ge(s["h1_done"], b + B)
                nc.sync.dma_start(h1_now[:].rearrange("p t d -> p (t d)"), h2_saved[b]).then_inc(s["h2_now"], 16)

            def send(b):
                sp.wait_ge(s["out_ready"], b * NT + NT)
                nc.sync.dma_start(out[b].rearrange("(t p) d -> p t d", p=P), h2[:]).then_inc(s["out_sent"], 16)
                sp.wait_ge(s["out_sent"], b * 16 + 16)
                nc.sync.sem_inc(s["sent"], 1)

            load_saved(0)
            with nc.sync.Fori(1, B) as b:
                load_saved(b)
                send(b - 1)
            send(B - 1)

        @block.gpsimd
        def _(pool):
            pool = Alone(nc.gpsimd, s["pool_waits"])

            nc.gpsimd.memset(mixed[:], 0.0)
            nc.gpsimd.memset(x0[:], 1.0)
            nc.gpsimd.memset(x1[:], 1.0)
            nc.gpsimd.memset(ones[:], 1.0)
            nc.gpsimd.memset(eps[:], EPS)
            nc.gpsimd.memset(grads[:], 0.0)
            nc.gpsimd.memset(xt[:], 1.0).then_inc(s["prep"], 1)

            with nc.gpsimd.Fori(0, B) as b:
                for t in range(NT):
                    pool.wait_ge(s["next_ready"], b * NT + t + 1)
                    nc.gpsimd.tensor_copy(idx_now[:, tile(t)], idx_next[:, tile(t)]).then_inc(s["idx_taken"], 1)
                    pool.wait_ge(s["idx_taken"], b * NT + t + 1)
                    for g in range(GROUPS):
                        pool.wait_ge(s["freed"], b * (NT * GROUPS) + (t * GROUPS + g + 1))
                        for j in range(PER):
                            n = g * PER + j
                            nc.gpsimd.indirect_dma_start(
                                rows[:, n, :], None, kv_table,
                                bass.IndirectOffsetOnAxis(ap=idx_now[:, t * P + n:t * P + n + 1], axis=0),
                            ).then_inc(got[g], 16)

        @block.tensor
        def _(pe):
            pe = Alone(nc.tensor, s["pe_waits"])

            mm, tr = nc.tensor.matmul, nc.tensor.transpose

            def turned(done):
                for t in range(NT):
                    last = tr(turn[0:D, 0, tile(t)], nrm[:, t, :], ident[0:P, 0:P])
                last.then_inc(done, 1)

            def prepare(b):
                pe.wait_ge(s["x_in"], b * 16 + 16)
                for n, (w, src) in enumerate([(win_s[:, 0], x_in), (win_s[:, 1], 0), (wout_s[:, 1], 1), (wout_s[:, 0], 0)]):
                    if n == 1:
                        pe.wait_ge(s["tok_act"], b * 4 + 1)
                    if n == 2:
                        pe.wait_ge(s["tok_sq"], b + 1)
                    if n == 3:
                        pe.wait_ge(s["tok_act"], b * 4 + 3)
                    for c in range(2):
                        rhs = x_in[:, c * HALF:(c + 1) * HALF] if n == 0 else tok[:, src, c, :]
                        last = mm(work[0:D, c, 0:HALF], w, rhs, start=True, stop=True)
                    last.then_inc(s["tok_mm"], 1)
                pe.wait_ge(s["tok_act"], b * 4 + 4)
                for t in range(NT):
                    for k in range(TAPS):
                        at = STRIDE * t * P + k
                        last = mm(work[0:P, 0, t * D:(t + 1) * D], mixed[:, at:at + STRIDE * (P - 1) + 1:STRIDE],
                                  tapdiag[:, k, :], start=(k == 0), stop=(k == TAPS - 1))
                last.then_inc(s["conv"], 1)
                pe.wait_ge(s["ln_n"], b * 2 + 1)
                turned(s["nT_mm"])
                pe.wait_ge(s["nT_done"], b * 2 + 1)
                for c in range(2):
                    mm(work[0:D, c, 0:S], wrope_s[:, c], nT[:], start=True, stop=True)
                    mm(sims[0:D, c, 0:S], wrope_s[:, 2 + c], nT[:], start=True, stop=True)
                for t in range(NT):
                    last = mm(turn[0:P, 0, t * D:(t + 1) * D], nT[:, tile(t)], wv_s[:], start=True, stop=True)
                last.then_inc(s["qk_mm"], 1)
                pe.wait_ge(s["rope_done"], b + 1)
                for j, dst in enumerate((work[0:P, 0], work[0:P, 1], sims[0:P, 0])):
                    last = mm(dst[:, 0:S - j * P], qk[:, 1, tile(j)], qk[:, 0, j * P:S], start=True, stop=True)
                last.then_inc(s["ret_mm"], 1)
                pe.wait_ge(s["ret_done"], b + 1)
                pe.wait_ge(s["v_done"], b + 1)
                for i in range(NT):
                    for j in range(i + 1):
                        last = mm(turn[0:P, 0, i * D:(i + 1) * D], ret[:, j, tile(i - j)], v_s[:, j, :],
                                  start=(j == 0), stop=(j == i))
                last.then_inc(s["mix_mm"], 1)
                pe.wait_ge(s["ln_n"], b * 2 + 2)
                turned(s["nT_mm"])

            def similarities(b, t):
                if t == 0:
                    pe.wait_ge(s["nT_done"], b * 2 + 2)
                else:
                    pe.wait_ge(s["sim_read"], b * NT + t)
                for c in range(2):
                    last = mm(sims[0:P, c, :], n2T[:, tile(t)], simw[:, c * 512:(c + 1) * 512], start=True, stop=True)
                last.then_inc(s["sim_mm"], 1)

            def turn_picks(b, t):
                pe.wait_ge(s["wgt_done"], b * NT + t + 1)
                tr(turn[:, 0, 0:P], wgt[:].rearrange("p h k -> p (h k)"), ident[0:P, 0:P])
                tr(turn[:, 0, P:2 * P], idxf[:].rearrange("p h k -> p (h k)"), ident[0:P, 0:P]).then_inc(s["tw_mm"], 1)

            def take_rows(b, t):
                pe.wait_ge(s["wbd_done"], b * NT + t + 1)
                for g in range(GROUPS):
                    pe.wait_ge(got[g], b * (NT * PER * 16) + (t + 1) * PER * 16)
                    if g == 0:
                        pe.wait_ge(s["kv_done"], b * NT + t + 1)
                    for j in range(PER):
                        n = g * PER + j
                        last = mm(gath[:, n // 64, (n % 64) * H:(n % 64 + 1) * H], rows[:, n, :], wbd[:, t * P + n, :],
                                  start=True, stop=True)
                    last.then_inc(s["freed"], 1)

            def attention(b):
                pe.wait_ge(s["kv_done"], b * NT + NT + 1)
                for j in range(NT):
                    if j >= 1:
                        pe.wait_ge(s["vo_done"], b * NT + j)
                    for h in range(H):
                        last = mm(work[0:P, 0, h * D:(h + 1) * D], kvT[D:128, h, tile(j)], wo_s[D:128, h, :],
                                  start=True, stop=True)
                    last.then_inc(s["vo_mm"], 1)
                pe.wait_ge(s["vo_done"], b * NT + NT)
                def queries(h):
                    mm(work[0:D, 0, 0:S], wq_s[:, h], n2T_now[:], start=True, stop=True).then_inc(s["q_mm"], 1)

                def scores(h):
                    pe.wait_ge(s["q_done"], b * H + h + 1)
                    if h >= 1:
                        pe.wait_ge(s["s_masked"], b * H + h)
                    for i, dst in enumerate((sims[0:P, 0, 0:P], sims[0:P, 0, P:S], sims[0:P, 1, 0:S])):
                        last = mm(dst, qT[:, h % 2, tile(i)], kvT[0:D, h, 0:(i + 1) * P], start=True, stop=True)
                    last.then_inc(s["s_mm"], 1)

                queries(0)
                scores(0)
                queries(1)
                for h in range(H):
                    pe.wait_ge(s["s_norm"], b * H + h + 1)
                    for c, (i, j, at) in enumerate(PAIRS):
                        dst = work[0:P, 1, at:at + P] if c < 3 else turn[0:P, 0, at:at + P]
                        last = tr(dst, prob[h % 2][:, c // 3, at:at + P], ident[0:P, 0:P])
                    last.then_inc(s["pT_mm"], 1)
                    if h + 1 < H:
                        scores(h + 1)
                    if h + 2 < H:
                        queries(h + 2)
                    pe.wait_ge(s["pT_done"], b * H + h + 1)
                    for c, (i, j, at) in enumerate(PAIRS):
                        last = mm(accu[0:P, 0, i * D:(i + 1) * D], pT[:, c // 3, at:at + P], vo[:, j, h * D:(h + 1) * D],
                                  start=(h == 0 and c == 0), stop=(h == H - 1 and c == 5), skip_group_check=True)
                last.then_inc(s["o_mm"], 1)

            def gradient(b):
                pe.wait_ge(s["ml_n"], b + 1)
                turned(s["nTm_mm"])
                pe.wait_ge(s["nTm_done"], b + 1)
                mm(work[0:D, 0, 0:S], mk_s[:], n3T[:], start=True, stop=True)
                mm(work[0:D, 1, 0:S], mv_s[:], n3T[:], start=True, stop=True)
                mm(sims[0:D, 0, 0:S], mlrb[:], n3T[:], start=True, stop=True).then_inc(s["x0_mm"], 1)
                pe.wait_ge(s["x0_done"], b + 1)
                mm(sims[0:D, 1, 0:S], params[0:D, 0, :], x0[0:D, :], start=True, stop=True).then_inc(s["z_mm"], 1)
                pe.wait_ge(s["x_done"], b * 2 + 1)
                mm(turn[0:D, 0, 0:S], params[0:D, 1, :], x1[0:D, :], start=True, stop=True).then_inc(s["z_mm"], 1)
                pe.wait_ge(s["dz2_done"], b + 1)
                mm(work[0:D, 0, 0:S], w1T_s[:], dz[:, 1, :], start=True, stop=True).then_inc(s["dx_mm"], 1)
                pe.wait_ge(s["dz_done"], b + 1)
                for l in range(2):
                    for t in range(NT):
                        tr(sims[0:P, l, t * D:(t + 1) * D], (x0, x1)[l][0:D, tile(t)], ident[0:D, 0:D])
                        last = tr(sims[0:P, l, 192 + t * D:192 + (t + 1) * D], dz[:, l, tile(t)], ident[0:D, 0:D])
                last.then_inc(s["t_mm"], 1)
                pe.wait_ge(s["t_done"], b + 1)
                for l in range(2):
                    for t in range(NT):
                        last = mm(accu[0:D + 1, 0, 256 + l * D:256 + (l + 1) * D], xt[:, l, t, :], dzt[:, l, t, :],
                                  start=(t == 0), stop=(t == NT - 1))
                last.then_inc(s["g_mm"], 1)

            def retrieve(b, chosen):
                pe.wait_ge(s["n3_now"], b * 16 + 16)
                mm(work[0:D, 0, 0:S], mq_s[:], n2T[:], start=True, stop=True).then_inc(s["x0_mm"], 1)
                if chosen:
                    logits(b - 1)
                pe.wait_ge(s["x0_done"], b + (B + 1))
                mm(sims[0:D, 0, 0:S], upd[:, 2, 0:D], x0[:], start=True, stop=True).then_inc(s["z_mm"], 1)
                if chosen:
                    experts(b - 1, 0)
                pe.wait_ge(s["x_done"], b * 2 + (2 * B + 1))
                mm(sims[0:D, 1, 0:S], upd[:, 2, D:2 * D], x1[:], start=True, stop=True).then_inc(s["z_mm"], 1)
                if chosen:
                    experts(b - 1, 1)
                    experts(b - 1, 2)
                pe.wait_ge(s["x_done"], b * 2 + (2 * B + 2))
                for t in range(NT):
                    last = tr(work[0:P, 1, t * D:(t + 1) * D], x2[:, tile(t)], ident[0:D, 0:D])
                last.then_inc(s["t_mm"], 1)
                pe.wait_ge(s["ml_n"], b + (B + 1))
                turned(s["nTm_mm"])
                pe.wait_ge(s["nTm_done"], b + (B + 1))
                for c in range(HID // 128):
                    last = mm(sims[:, c, 0:S], fw1_s[:, c * 128:(c + 1) * 128], nT[:], start=True, stop=True)
                last.then_inc(s["h_mm"], 1)

            def logits(b):
                pe.wait_ge(s["h_act"], b + 1)
                for t in range(NT):
                    dst = accu[0:P, 0, t * E:(t + 1) * E]
                    mm(dst, ones[:], fbg_s[:], start=True, stop=False)
                    for c in range(HID // 128):
                        last = mm(dst, hid[:, c, tile(t)], fwg_s[:, c, :], start=False, stop=(c == HID // 128 - 1))
                last.then_inc(s["lg_mm"], 1)

            def experts(b, t):
                pe.wait_ge(s["wy"], b * NT + (t + 1))
                dst = gath[0:P, t % 2, :]
                mm(dst, ones[:], fbd_s[:], start=True, stop=False)
                for c in range(HID // 128):
                    last = mm(dst, hid[:, c, tile(t)], fwd_s[:, c, :], start=False, stop=(c == HID // 128 - 1))
                last.then_inc(s["y_mm"], 1)

            pe.wait_ge(s["loaded"], ALL_LOADED)
            pe.wait_ge(s["prep"], 1)
            nc.tensor.sem_inc(s["freed"], GROUPS)
            nc.tensor.sem_inc(s["kv_done"], 1)
            for ph in range(2 * H):
                last = mm(sims[0:D, ph // H, (ph % H) * SUB:(ph % H + 1) * SUB], pkq_s[:, ph, :], pkk_s[:, ph, :],
                          start=True, stop=True)
            last.then_inc(s["fold_mm"], 1)
            pe.wait_ge(s["fold_done"], 1)
            pe.wait_ge(s["tapd"], 1)
            prepare(0)
            for t in range(2):
                similarities(0, t)
                turn_picks(0, t)
            similarities(0, 2)
            take_rows(0, 0)
            turn_picks(0, 2)
            with nc.tensor.Fori(0, B - 1) as b:
                prepare(b + 1)
                for t in range(2):
                    similarities(b + 1, t)
                    take_rows(b, t + 1)
                    turn_picks(b + 1, t)
                attention(b)
                gradient(b)
                similarities(b + 1, 2)
                take_rows(b + 1, 0)
                turn_picks(b + 1, 2)
            for t in range(1, NT):
                take_rows(B - 1, t)
            attention(B - 1)
            gradient(B - 1)
            pe.wait_ge(s["upd_done"], 1)
            nc.tensor.sem_inc(s["wy"], 1)
            retrieve(0, False)
            with nc.tensor.Fori(1, B) as b:
                retrieve(b, True)
            logits(B - 1)
            for t in range(NT):
                experts(B - 1, t)


        @block.scalar
        def _(act):
            act = Alone(nc.scalar, s["act_waits"])

            fn = nc.scalar.activation

            def deviation(n, var_ready, std_done):
                act.wait_ge(var_ready, n)
                fn(std[:], mv[:, :, 1], ACT.Sqrt, bias=eps[:, 0:1]).then_inc(std_done, 1)

            def keep(b):
                if isinstance(b, int) and b == 0:
                    act.wait_ge(s["nT_done"], 2)
                nc.scalar.copy(h1_now[:], h1[:])
                nc.scalar.copy(n2T_now[:], n2T[:]).then_inc(s["kept"], 1)

            def prepare(b):
                for n, (dst, bias) in enumerate([(0, 0), (None, 1), (0, 3), (None, 2)]):
                    act.wait_ge(s["tok_mm"], b * 4 + n + 1)
                    if n == 3:
                        to = mixed[:, PAD:PAD + S_IN].rearrange("d (c t) -> d c t", c=2)
                    else:
                        to = tok[:, (0, 1, 0)[n]]
                    fn(to, work[0:D, :, 0:HALF], ACT.Tanh, bias=bias_s[:, bias:bias + 1]).then_inc(s["tok_act"], 1)
                deviation(b * 2 + 1, s["ln_var"], s["ln_std"])
                act.wait_ge(s["nT_mm"], b * 2 + 1)
                nc.scalar.copy(nT[:], turn[0:D, 0, 0:S]).then_inc(s["nT_done"], 1)
                act.wait_ge(s["qk_mm"], b + 1)
                nc.scalar.copy(v_s[:].rearrange("p t d -> p (t d)"), turn[0:P, 0, 0:NT * D]).then_inc(s["v_done"], 1)
                deviation(b * 2 + 2, s["ln_var"], s["ln_std"])
                act.wait_ge(s["nT_mm"], b * 2 + 2)
                nc.scalar.copy(n2T[:], turn[0:D, 0, 0:S]).then_inc(s["nT_done"], 1)

            def soften(b, t):
                act.wait_ge(s["fdiff"], b * NT + t + 1)
                fn(wgt[:], wgt[:], ACT.Exp).then_inc(s["fexp"], 1)

            def turn_weights(b, t):
                act.wait_ge(s["next_ready"], b * NT + t + 1)
                if not (isinstance(b, int) and b == 0):
                    act.wait_ge(s["wbd_done"], b * NT + (t + 1 - NT))
                nc.scalar.copy(wT_next[:, tile(t)], turn[:, 0, 0:P]).then_inc(s["wT_done"], 1)

            def take_rows(b, t):
                act.wait_ge(s["freed"], b * (NT * GROUPS) + (t * GROUPS + 2 * GROUPS))
                nc.scalar.copy(kvT[:, :, t * P:t * P + 64], gath[:, 0, :].rearrange("p (n h) -> p h n", h=H))
                nc.scalar.copy(kvT[:, :, t * P + 64:(t + 1) * P],
                               gath[:, 1, 0:(P - 64) * H].rearrange("p (n h) -> p h n", h=H)).then_inc(s["kv_done"], 1)

            def attention(b):
                for j in range(NT):
                    act.wait_ge(s["vo_mm"], b * NT + j + 1)
                    nc.scalar.copy(vo[:, j, :], work[0:P, 0, :]).then_inc(s["vo_done"], 1)
                def scale_q(h):
                    act.wait_ge(s["q_mm"], b * H + h + 1)
                    nc.scalar.mul(qT[:, h % 2], work[0:D, 0, 0:S], float(D) ** -0.5).then_inc(s["q_done"], 1)

                scale_q(0)
                scale_q(1)
                for h in range(H):
                    act.wait_ge(s["s_max"], b * H + h + 1)
                    for i, p in enumerate(regions(h)):
                        last = fn(p, p, ACT.Exp, bias=mx[:, h % 2, i:i + 1], accum_out=zs[:, h % 2, i:i + 1])
                    last.then_inc(s["s_exp"], 1)
                    act.wait_ge(s["pT_mm"], b * H + h + 1)
                    nc.scalar.copy(pT[:, 0, :], work[0:P, 1, 0:S])
                    nc.scalar.copy(pT[:, 1, :], turn[0:P, 0, 0:S]).then_inc(s["pT_done"], 1)
                    if h + 2 < H:
                        scale_q(h + 2)

            def gradient(b):
                deviation(b + 1, s["ml_var"], s["ml_std"])
                act.wait_ge(s["nTm_mm"], b + 1)
                act.wait_ge(s["saved"], b + 1)
                nc.scalar.copy(n3T[:], turn[0:D, 0, 0:S]).then_inc(s["nTm_done"], 1)
                act.wait_ge(s["x0_mm"], b + 1)
                nc.scalar.copy(x0[0:D, :], work[0:D, 0, 0:S]).then_inc(s["x0_done"], 1)
                fn(sg[:, 2, :], sims[0:D, 0, 0:S], ACT.Sigmoid, bias=mblr_s[:, 0:1]).then_inc(s["alr_done"], 1)
                for l, z in enumerate((sims[0:D, 1, 0:S], turn[0:D, 0, 0:S])):
                    act.wait_ge(s["z_mm"], b * 2 + l + 1)
                    fn(sg[:, l, :], z, ACT.Sigmoid, bias=mb_s[:, l:l + 1]).then_inc(s["sig_done"], 1)
                act.wait_ge(s["t_mm"], b + 1)
                for l in range(2):
                    nc.scalar.copy(xt[:, l, :, 0:D], sims[0:P, l, 0:192].rearrange("p (t d) -> p t d", d=D))
                    last = nc.scalar.copy(dzt[:, l, :, :], sims[0:P, l, 192:384].rearrange("p (t d) -> p t d", d=D))
                last.then_inc(s["t_done"], 1)

            def retrieve(b, chosen):
                act.wait_ge(s["x0_mm"], b + (B + 1))
                nc.scalar.copy(x0[0:D, :], work[0:D, 0, 0:S]).then_inc(s["x0_done"], 1)
                if chosen:
                    exp_logits(b - 1)
                for l in range(2):
                    act.wait_ge(s["z_mm"], b * 2 + (2 * B + l + 1))
                    fn(sg[:, l, :], sims[0:D, l, 0:S], ACT.Sigmoid).then_inc(s["sig_done"], 1)
                deviation(b + (B + 1), s["ml_var"], s["ml_std"])
                act.wait_ge(s["nTm_mm"], b + (B + 1))
                nc.scalar.copy(nT[:], turn[0:D, 0, 0:S]).then_inc(s["nTm_done"], 1)
                act.wait_ge(s["h_mm"], b + 1)
                for c in range(HID // 128):
                    last = fn(hid[:, c, :], sims[:, c, 0:S], ACT.Gelu, bias=fb1_s[:, c:c + 1])
                last.then_inc(s["h_act"], 1)

            def exp_logits(b):
                act.wait_ge(s["lg_d"], b + 1)
                fn(e8[:], e8[:], ACT.Exp).then_inc(s["lg_exp"], 1)

            act.wait_ge(s["loaded"], ALL_LOADED)
            act.wait_ge(s["prep"], 1)
            prepare(0)
            for t in range(2):
                soften(0, t)
                turn_weights(0, t)
            keep(0)
            soften(0, 2)
            take_rows(0, 0)
            turn_weights(0, 2)
            with nc.scalar.Fori(0, B - 1) as b:
                prepare(b + 1)
                for t in range(2):
                    soften(b + 1, t)
                    take_rows(b, t + 1)
                    turn_weights(b + 1, t)
                attention(b)
                gradient(b)
                keep(b + 1)
                soften(b + 1, 2)
                take_rows(b + 1, 0)
                turn_weights(b + 1, 2)
            for t in range(1, NT):
                take_rows(B - 1, t)
            attention(B - 1)
            gradient(B - 1)
            retrieve(0, False)
            with nc.scalar.Fori(1, B) as b:
                retrieve(b, True)
            exp_logits(B - 1)

        @block.vector
        def _(dve):
            dve = Alone(nc.vector, s["dve_waits"])

            v = nc.vector

            def normalise(src, n, gone, aggregated, deviated, inverted, normalised):
                for t in range(NT):
                    last = v.bn_stats(stats[:, t, :], src[:, t, :])
                last.then_inc(gone, 1)
                dve.wait_ge(gone, n)
                for t in range(NT):
                    last = v.bn_aggr(mv[:, t, :], stats[:, t, :])
                last.then_inc(aggregated, 1)
                dve.wait_ge(deviated, n)
                v.reciprocal(rstd[:], std[:]).then_inc(inverted, 1)
                dve.wait_ge(inverted, n)
                for t in range(NT):
                    last = v.tensor_scalar(nrm[:, t, :], src[:, t, :], mv[:, t, 0:1], rstd[:, t:t + 1],
                                           ALU.subtract, ALU.mult)
                last.then_inc(normalised, 1)

            def prepare(b):
                dve.wait_ge(s["tok_act"], b * 4 + 2)
                for c in range(2):
                    last = v.scalar_tensor_tensor(tok[:, 1, c, :], tok[:, 1, c, :], core_s[:, 0:1], tok[:, 1, c, :],
                                                  ALU.mult, ALU.mult)
                last.then_inc(s["tok_sq"], 1)
                dve.wait_ge(s["conv"], b + 1)
                v.tensor_copy(h0[:].rearrange("p t d -> p (t d)"), work[0:P, 0, 0:NT * D]).then_inc(s["h0_done"], 1)
                dve.wait_ge(s["h0_done"], b + 1)
                normalise(h0, b * 2 + 1, s["ln_stats"], s["ln_var"], s["ln_std"], s["ln_inv"], s["ln_n"])
                dve.wait_ge(s["qk_mm"], b + 1)
                v.tensor_tensor(qk[:], work[0:D, :, 0:S], rope_t[:, 0], ALU.mult).then_inc(s["rope_a"], 1)
                v.tensor_tensor(qk_b, sims[0:D, :, 0:S], rope_t[:, 1], ALU.mult).then_inc(s["rope_b"], 1)
                dve.wait_ge(s["rope_a"], b + 1)
                dve.wait_ge(s["rope_b"], b + 1)
                v.tensor_tensor(qk[:], qk[:], qk_b, ALU.add).then_inc(s["rope_done"], 1)
                dve.wait_ge(s["ret_mm"], b + 1)
                for j, src in enumerate((work[0:P, 0], work[0:P, 1], sims[0:P, 0])):
                    last = v.tensor_tensor(ret[:, j, 0:S - j * P], src[:, 0:S - j * P], decay[:, 0:S - j * P], ALU.mult)
                last.then_inc(s["ret_done"], 1)
                dve.wait_ge(s["mix_mm"], b + 1)
                if not (isinstance(b, int) and b == 0):
                    dve.wait_ge(s["kept"], b)
                v.tensor_tensor(h1[:].rearrange("p t d -> p (t d)"), h0[:].rearrange("p t d -> p (t d)"),
                                turn[0:P, 0, 0:NT * D], ALU.add).then_inc(s["h1_done"], 1)
                dve.wait_ge(s["h1_done"], b + 1)
                normalise(h1, b * 2 + 2, s["ln_stats"], s["ln_var"], s["ln_std"], s["ln_inv"], s["ln_n"])

            def pick_rows(b, t):
                n = b * NT + t + 1
                dve.wait_ge(s["sim_mm"], n)
                sim = sims[0:P].rearrange("p c (g k) -> p (c g) k", k=SUB)
                for g in range(2 * H):
                    last = v.max(s16[:, g, 0:8], sim[:, g, :])
                last.then_inc(s["top_a"], 1)
                dve.wait_ge(s["top_a"], n)
                for g in range(2 * H):
                    v.max_index(i16[:, g, 0:8], s16[:, g, 0:8], sim[:, g, :])
                    last = v.match_replace(rest[:, g, :], s16[:, g, 0:8], sim[:, g, :], LOWEST)
                last.then_inc(s["sim_read"], 1)
                dve.wait_ge(s["sim_read"], n)
                for g in range(2 * H):
                    last = v.max(s16[:, g, 8:16], rest[:, g, :])
                last.then_inc(s["top_b"], 1)
                dve.wait_ge(s["top_b"], n)
                for g in range(2 * H):
                    last = v.max_index(i16[:, g, 8:16], s16[:, g, 8:16], rest[:, g, :])
                last.then_inc(s["top_c"], 1)
                dve.wait_ge(s["top_c"], n)
                v.tensor_copy(i16f[:, 0:H], i16[:, 0:H])
                v.scalar_tensor_tensor(i16f[:, H:], i16[:, H:], float(SUB), headoff[:], ALU.mult,
                                       ALU.add).then_inc(s["top_d"], 1)
                dve.wait_ge(s["top_d"], n)
                for src, dst, signal in ((s16, cand, s["cand_a"]), (i16f, cidx, s["cand_b"])):
                    for (a, m), off in zip(RUNS, OFFS):
                        v.tensor_tensor(dst[:, :, off:off + m], src[:, H:, 0:m],
                                        src[:, 0:H, a:a + 1].broadcast_to([P, H, m]), ALU.add)
                    v.tensor_tensor(dst[:, :, TAIL_AT:], src[:, 0:H, K // 2:K],
                                    src[:, H:, 0:1].broadcast_to([P, H, K // 2]), ALU.add).then_inc(signal, 1)
                dve.wait_ge(s["cand_a"], n)
                for h in range(H):
                    last = v.max(f16[:, h, 0:8], cand[:, h, :])
                last.then_inc(s["fin_a"], 1)
                dve.wait_ge(s["fin_a"], n)
                for h in range(H):
                    v.max_index(pos[:, h, 0:8], f16[:, h, 0:8], cand[:, h, :])
                    last = v.match_replace(crest[:, h, :], f16[:, h, 0:8], cand[:, h, :], LOWEST)
                last.then_inc(s["fin_b"], 1)
                dve.wait_ge(s["fin_b"], n)
                for h in range(H):
                    last = v.max(f16[:, h, 8:16], crest[:, h, :])
                last.then_inc(s["fin_c"], 1)
                dve.wait_ge(s["fin_c"], n)
                v.tensor_tensor(wgt[:], f16[:], f16[:, :, 0:1].broadcast_to([P, H, K]),
                                ALU.subtract).then_inc(s["fdiff"], 1)
                for h in range(H):
                    last = v.max_index(pos[:, h, 8:16], f16[:, h, 8:16], crest[:, h, :])
                last.then_inc(s["fin_d"], 1)
                dve.wait_ge(s["fin_d"], n)
                v.tensor_copy(posf[:], pos[:]).then_inc(s["pos_f"], 1)
                dve.wait_ge(s["pos_f"], n)
                dve.wait_ge(s["cand_b"], n)
                for c in range(H // HH):
                    at = slice(c * HH, (c + 1) * HH)
                    m = b * (NT * (H // HH)) + (t * (H // HH) + c + 1)
                    v.tensor_tensor(pick,
                                    posf[:, at].rearrange("p h k -> p (h k)").unsqueeze(2).broadcast_to([P, HH * K, CAND]),
                                    iota[:].unsqueeze(1).broadcast_to([P, HH * K, CAND]),
                                    ALU.is_equal).then_inc(s["pick_a"], 1)
                    dve.wait_ge(s["pick_a"], m)
                    four = pick.rearrange("p (h k) c -> p h k c", k=K)
                    v.tensor_tensor(four, four, cidx[:, at].unsqueeze(2).broadcast_to([P, HH, K, CAND]),
                                    ALU.mult).then_inc(s["pick_b"], 1)
                    dve.wait_ge(s["pick_b"], m)
                    v.tensor_reduce(idxf[:, at].rearrange("p h k -> p (h k)"), pick, AX_X,
                                    ALU.add).then_inc(s["pick_c"], 1)
                    dve.wait_ge(s["pick_c"], m)
                dve.wait_ge(s["fexp"], n)
                v.tensor_reduce(esum[:, 0, :], wgt[:], AX_X, ALU.add).then_inc(s["fsum"], 1)
                dve.wait_ge(s["fsum"], n)
                v.reciprocal(esum[:, 1, :], esum[:, 0, :]).then_inc(s["frec"], 1)
                dve.wait_ge(s["frec"], n)
                v.tensor_tensor(wgt[:], wgt[:], esum[:, 1, :].unsqueeze(2).broadcast_to([P, H, K]),
                                ALU.mult).then_inc(s["wgt_done"], 1)
                dve.wait_ge(s["tw_mm"], n)
                if not (isinstance(b, int) and b == 0):
                    dve.wait_ge(s["idx_taken"], b * NT + (t + 1 - NT))
                v.tensor_copy(idx_next[:, tile(t)], turn[:, 0, P:2 * P]).then_inc(s["next_ready"], 1)

            def spread_weights(b, t):
                dve.wait_ge(s["wT_done"], b * NT + t + 1)
                v.tensor_tensor(wbd[:, tile(t)], wT_next[:, tile(t)].unsqueeze(2).broadcast_to([128, P, H]),
                                headmask[:].unsqueeze(1).broadcast_to([128, P, H]), ALU.mult).then_inc(s["wbd_done"], 1)

            def attention(b):
                def softmax_max(h):
                    n = b * H + h + 1
                    dve.wait_ge(s["s_mm"], n)
                    v.tensor_tensor(prob[h % 2], sims[0:P, :, 0:S], mask[:], ALU.add).then_inc(s["s_masked"], 1)
                    dve.wait_ge(s["s_masked"], n)
                    for i, p in enumerate(regions(h)):
                        last = v.tensor_reduce(mx[:, h % 2, i:i + 1], p, AX_X, ALU.max, negate=True)
                    last.then_inc(s["s_max"], 1)

                softmax_max(0)
                for h in range(H):
                    n = b * H + h + 1
                    dve.wait_ge(s["s_exp"], n)
                    v.reciprocal(zs[:, 2 + h % 2, 0:NT], zs[:, h % 2, 0:NT]).then_inc(s["s_rec"], 1)
                    dve.wait_ge(s["s_rec"], n)
                    for i, p in enumerate(regions(h)):
                        last = v.tensor_scalar(p, p, zs[:, 2 + h % 2, i:i + 1], None, ALU.mult)
                    last.then_inc(s["s_norm"], 1)
                    if h + 1 < H:
                        softmax_max(h + 1)
                dve.wait_ge(s["o_mm"], b + 1)
                if not (isinstance(b, int) and b == 0):
                    dve.wait_ge(s["saved"], b + 1)
                v.tensor_tensor(h2[:].rearrange("p t d -> p (t d)"), h1_now[:].rearrange("p t d -> p (t d)"),
                                accu[0:P, 0, 0:NT * D], ALU.add).then_inc(s["h2_done"], 1)
                dve.wait_ge(s["h2_done"], b + 1)

            def gradient(b):
                normalise(h2, b + 1, s["ml_stats"], s["ml_var"], s["ml_std"], s["ml_inv"], s["ml_n"])
                for l, (z, xin, xout) in enumerate(((sims[0:D, 1, 0:S], x0[0:D], x1[0:D]), (turn[0:D, 0, 0:S], x1[0:D], x2[:]))):
                    n = b * 2 + l + 1
                    dve.wait_ge(s["sig_done"], n)
                    if l == 0:
                        dve.wait_ge(s["x0_done"], b + 1)
                    v.scalar_tensor_tensor(s_a[:, l, :], z, mb_s[:, l:l + 1], sg[:, l, :], ALU.add,
                                           ALU.mult).then_inc(s["silu_a"], 1)
                    dve.wait_ge(s["silu_a"], n)
                    v.tensor_tensor(xout, xin, s_a[:, l, :], ALU.add).then_inc(s["x_done"], 1)
                    v.scalar_tensor_tensor(d_a[:, l, :], s_a[:, l, :], 1.0, sg[:, l, :], ALU.subtract,
                                           ALU.mult).then_inc(s["dd_a"], 1)
                    dve.wait_ge(s["dd_a"], n)
                    v.tensor_tensor(d_a[:, l, :], s_a[:, l, :], d_a[:, l, :], ALU.subtract).then_inc(s["d_done"], 1)
                dve.wait_ge(s["x_done"], b * 2 + 2)
                v.tensor_tensor(x2[:], x2[:], work[0:D, 1, 0:S], ALU.subtract).then_inc(s["err_a"], 1)
                dve.wait_ge(s["err_a"], b + 1)
                dve.wait_ge(s["alr_done"], b + 1)
                v.scalar_tensor_tensor(g2, x2[:], ALR_SCALE, sg[:, 2, :], ALU.mult, ALU.mult).then_inc(s["g2_done"], 1)
                dve.wait_ge(s["g2_done"], b + 1)
                dve.wait_ge(s["d_done"], b * 2 + 2)
                v.tensor_tensor(dz[:, 1, :], g2, d_a[:, 1, :], ALU.mult).then_inc(s["dz2_done"], 1)
                dve.wait_ge(s["dx_mm"], b + 1)
                v.tensor_tensor(g2, g2, work[0:D, 0, 0:S], ALU.add).then_inc(s["g1_done"], 1)
                dve.wait_ge(s["g1_done"], b + 1)
                v.tensor_tensor(dz[:, 0, :], g2, d_a[:, 0, :], ALU.mult).then_inc(s["dz_done"], 1)
                dve.wait_ge(s["g_mm"], b + 1)
                v.tensor_tensor(grads[:], grads[:], accu[0:D + 1, 0, 256:256 + 2 * D], ALU.add).then_inc(s["g_done"], 1)

            def retrieve(b, chosen):
                if chosen:
                    choose(b - 1)
                for l, (xin, xout) in enumerate(((x0[0:D], x1[0:D]), (x1[0:D], x2[:]))):
                    n = b * 2 + (2 * B + l + 1)
                    dve.wait_ge(s["sig_done"], n)
                    if l == 0:
                        dve.wait_ge(s["x0_done"], b + (B + 1))
                    v.tensor_tensor(s_a[:, l, :], sims[0:D, l, 0:S], sg[:, l, :], ALU.mult).then_inc(s["silu_a"], 1)
                    dve.wait_ge(s["silu_a"], n)
                    v.tensor_tensor(xout, xin, s_a[:, l, :], ALU.add).then_inc(s["x_done"], 1)
                    if chosen:
                        apply_choice(b - 1, l)
                if chosen:
                    apply_choice(b - 1, 2)
                    dve.wait_ge(s["out_ready"], b * NT)
                dve.wait_ge(s["t_mm"], b + (B + 1))
                dve.wait_ge(s["h2_now"], b * 16 + 16)
                v.tensor_tensor(h1[:].rearrange("p t d -> p (t d)"), h1_now[:].rearrange("p t d -> p (t d)"),
                                work[0:P, 1, 0:NT * D], ALU.add).then_inc(s["h1_done"], 1)
                dve.wait_ge(s["h1_done"], b + (B + 1))
                normalise(h1, b + (B + 1), s["ml_stats"], s["ml_var"], s["ml_std"], s["ml_inv"], s["ml_n"])

            def choose(b):
                n = b + 1
                lg = accu[0:P, 0, 0:NT * E].rearrange("p (t e) -> p t e", e=E)
                dve.wait_ge(s["lg_mm"], n)
                v.tensor_reduce(lmax[:, 0, :], lg, AX_X, ALU.max).then_inc(s["lg_max"], 1)
                dve.wait_ge(s["lg_max"], n)
                v.tensor_tensor(e8[:], lg, lmax[:, 0, :].unsqueeze(2).broadcast_to([P, NT, E]),
                                ALU.subtract).then_inc(s["lg_d"], 1)
                dve.wait_ge(s["lg_exp"], n)
                v.tensor_reduce(lmax[:, 1, :], e8[:], AX_X, ALU.add).then_inc(s["lg_sum"], 1)
                dve.wait_ge(s["lg_sum"], n)
                v.reciprocal(lmax[:, 2, :], lmax[:, 1, :]).then_inc(s["lg_rec"], 1)
                dve.wait_ge(s["lg_rec"], n)
                v.tensor_tensor(p8[:], e8[:], lmax[:, 2, :].unsqueeze(2).broadcast_to([P, NT, E]),
                                ALU.mult).then_inc(s["lg_p"], 1)
                dve.wait_ge(s["lg_p"], n)
                for t in range(NT):
                    last = v.max(m8[:, t, :], p8[:, t, :])
                last.then_inc(s["lg_top"], 1)
                dve.wait_ge(s["lg_top"], n)
                for t in range(NT):
                    last = v.max_index(mi8[:, t, :], m8[:, t, :], p8[:, t, :])
                last.then_inc(s["lg_i"], 1)
                dve.wait_ge(s["lg_i"], n)
                v.tensor_copy(mif[:], mi8[:, :, 0]).then_inc(s["lg_if"], 1)
                dve.wait_ge(s["lg_if"], n)
                v.tensor_tensor(c8[:], iota[:, 0:E].unsqueeze(1).broadcast_to([P, NT, E]),
                                mif[:].unsqueeze(2).broadcast_to([P, NT, E]), ALU.is_equal).then_inc(s["lg_oh"], 1)
                dve.wait_ge(s["lg_oh"], n)
                v.tensor_tensor(c8[:], c8[:], p8[:], ALU.mult).then_inc(s["lg_c"], 1)
                dve.wait_ge(s["lg_c"], n)

            def apply_choice(b, t):
                n = b * NT + t + 1
                dve.wait_ge(s["y_mm"], n)
                v.tensor_tensor(wy, gath[0:P, t % 2, :].rearrange("p (e d) -> p e d", e=E),
                                c8[:, t, :].unsqueeze(2).broadcast_to([P, E, D]), ALU.mult).then_inc(s["wy"], 1)
                dve.wait_ge(s["wy"], n + 1)
                v.tensor_reduce(ysum[:], wy.rearrange("p e d -> p d e"), AX_X, ALU.add).then_inc(s["wy_sum"], 1)
                dve.wait_ge(s["wy_sum"], n)
                if t == 0:
                    dve.wait_ge(s["sent"], b + 1)
                v.tensor_tensor(h2[:, t, :], h1[:, t, :], ysum[:], ALU.add).then_inc(s["out_ready"], 1)

            dve.wait_ge(s["loaded"], ALL_LOADED)
            dve.wait_ge(s["prep"], 1)
            v.tensor_scalar(core_s[:, 1:2], core_s[:, 0:1], -1.0, None, ALU.mult).then_inc(s["upd_a"], 1)
            dve.wait_ge(s["upd_a"], 1)
            v.tensor_tensor(core_s[:, 0:1], core_s[:, 0:1], core_s[:, 1:2], ALU.max)
            v.tensor_copy(mlrb[:], mlr_s[:].broadcast_to([D, D]))
            for k in range(TAPS):
                last = v.tensor_scalar(tapdiag[:, k, :], ident[0:D, 0:D], taps_s[:, k:k + 1], None, ALU.mult)
            last.then_inc(s["tapd"], 1)
            dve.wait_ge(s["tapd"], 1)
            dve.wait_ge(s["fold_mm"], 1)
            v.tensor_copy(simw[:], sims[0:D].rearrange("p c k -> p (c k)")).then_inc(s["fold_done"], 1)
            prepare(0)
            for t in range(2):
                pick_rows(0, t)
                spread_weights(0, t)
            pick_rows(0, 2)
            spread_weights(0, 2)
            with nc.vector.Fori(0, B - 1) as b:
                prepare(b + 1)
                for t in range(2):
                    pick_rows(b + 1, t)
                attention(b)
                gradient(b)
                for t in range(2):
                    spread_weights(b + 1, t)
                pick_rows(b + 1, 2)
                spread_weights(b + 1, 2)
            attention(B - 1)
            gradient(B - 1)
            dve.wait_ge(s["g_done"], B)
            v.tensor_scalar(upd[:, 0, :], grads[:], -1.0, None, ALU.mult).then_inc(s["upd_b"], 1)
            dve.wait_ge(s["upd_b"], 1)
            v.tensor_tensor(upd[:, 0, :], upd[:, 0, :], grads[:], ALU.max).then_inc(s["upd_b"], 1)
            dve.wait_ge(s["upd_b"], 2)
            v.tensor_scalar(upd[:, 0, :], upd[:, 0, :], GEPS, None, ALU.add).then_inc(s["upd_c"], 1)
            dve.wait_ge(s["upd_c"], 1)
            v.reciprocal(upd[:, 1, :], upd[:, 0, :]).then_inc(s["upd_d"], 1)
            dve.wait_ge(s["upd_d"], 1)
            v.scalar_tensor_tensor(upd[:, 1, :], upd[:, 1, :], LR, grads[:], ALU.mult, ALU.mult).then_inc(s["upd_e"], 1)
            dve.wait_ge(s["upd_e"], 1)
            v.scalar_tensor_tensor(upd[:, 2, :], params[:].rearrange("p l d -> p (l d)"), 1.0 - LR * WD, upd[:, 1, :],
                                   ALU.mult, ALU.subtract).then_inc(s["upd_done"], 1)
            retrieve(0, False)
            with nc.vector.Fori(1, B) as b:
                retrieve(b, True)
            choose(B - 1)
            for t in range(NT):
                apply_choice(B - 1, t)


def tables():
    f = np.float32
    inv = f(1.0) / f(10000.0) ** (np.arange(0, D, 2, dtype=f) / f(D))
    pos = np.arange(S, dtype=f)
    ang = (pos[:, None] * inv[None, :]).astype(f)
    base = (np.arange(0, D, 2, dtype=f) + f(0.4 * D)) / f(1.4 * D)
    scale = base[None, :] ** (pos[:, None] / f(512.0))
    rope = np.zeros((D, 2, 2, S), f)
    for n, by in enumerate((scale, f(1.0) / scale)):
        c, sn = (np.cos(ang) * by).T, (np.sin(ang) * by).T
        rope[:, 0, n] = np.concatenate([c, c])
        rope[:, 1, n] = np.concatenate([-sn, sn])
    ahead = np.arange(S)[None, :] - np.arange(P)[:, None]
    decay = np.where(ahead >= 0, f(0.96875) ** np.maximum(ahead, 0).astype(f), f(0)).astype(f)
    hidden = np.where(np.arange(P)[None, :] > np.arange(P)[:, None], f(LOWEST), f(0))
    mask = np.zeros((P, 2, S), f)
    mask[:, 0, 0:P] = hidden
    mask[:, 0, 2 * P:] = hidden
    mask[:, 1, 2 * P:] = hidden
    iota = np.tile(np.arange(CAND, dtype=f), (P, 1))
    headoff = np.tile((np.arange(H, dtype=f) * NKV)[None, :, None], (P, 1, K))
    headmask = (np.arange(128)[:, None] // K == np.arange(H)[None, :]).astype(f)
    return [rope, decay, mask, np.eye(128, dtype=f), iota, headoff, headmask]


def kernel(**inputs):
    import concourse.bacc as bacc
    from concourse.bass_utils import run_bass_kernel_spmd as run

    a = {k: np.ascontiguousarray(v) for k, v in inputs.items()}
    wq, wk = a["L0_attn_W_Q"], a["L0_attn_W_K"]
    even_odd = lambda w: np.concatenate([w[:, 0::2], w[:, 1::2]], 1)
    odd_even = lambda w: np.concatenate([w[:, 1::2], w[:, 0::2]], 1)
    feeds = [
        a["x"].transpose(0, 2, 1),
        a["L0_tok_W_in"], a["L0_tok_b_in"].T, a["L0_tok_W_out"], a["L0_tok_b_out"].T, a["L0_tok_core_diag"],
        a["L0_tok_conv_filter"],
        np.stack([even_odd(wq), even_odd(wk), odd_even(wq), odd_even(wk)], 1), a["L0_attn_W_V"],
        a["L0_ffn_Wq_pk"].reshape(D, 2 * H, D // 2).transpose(2, 1, 0),
        a["L0_ffn_pk_keys"].transpose(3, 0, 2, 1).reshape(D // 2, 2 * H, SUB),
        a["L0_ffn_Wq"], np.concatenate([a["L0_ffn_keys_table"], a["L0_ffn_values_table"]], 1), a["L0_ffn_Wo"],
        a["L1_attn_Wk"], a["L1_attn_Wq"], a["L1_attn_Wv"], a["L1_attn_Wlr"], a["L1_attn_blr"],
        np.concatenate([a["L1_attn_Ws"], a["L1_attn_bs"][:, None, :]], 1).transpose(1, 0, 2), a["L1_attn_bs"].T,
        a["L1_attn_Ws"][1].T,
        a["L1_ffn_W1"], a["L1_ffn_b1"].reshape(HID // 128, 128).T, a["L1_ffn_Wg"], a["L1_ffn_bg"],
        a["L1_ffn_Wd"].reshape(E, HID // 128, 128, D).transpose(2, 1, 0, 3).reshape(128, HID // 128, E * D),
        a["L1_ffn_bd"].reshape(1, E * D),
    ] + tables()
    nc = bacc.Bacc("TRN2", target_bir_lowering=False, num_devices=1)
    arrays, args = {}, []
    for n, x in enumerate(feeds):
        arrays[f"in_{n}"] = np.ascontiguousarray(x)
        args.append(nc.dram_tensor(f"in_{n}", x.shape, F32, kind="ExternalInput").ap())
    args.append(nc.dram_tensor("out", (B, S, D), F32, kind="ExternalOutput").ap())
    tower(nc, *args)
    return run(nc, [arrays], core_ids=[0]).results[0]["out"]
```

```python
from contextlib import ExitStack

import numpy as np

import concourse.bass as bass
from concourse import mybir

F32 = mybir.dt.float32
U32 = mybir.dt.uint32
ALU = mybir.AluOpType
ACT = mybir.ActivationFunctionType
AX_X = mybir.AxisListType.X

B, S_IN, D = 16, 750, 64
TAPS, STRIDE = 15, 2
PAD = TAPS // 2
S = (S_IN + 2 * PAD - TAPS) // STRIDE + 1
P = 125
NT = S // P
HALF = S_IN // 2
H, K, SUB = 8, 16, 64
SLOTS = H * K
NKV = SUB * SUB
RUNS = [(a, K // (a + 1)) for a in range(K // 2)]
TAIL_AT = sum(n for _, n in RUNS)
CAND = TAIL_AT + K - K // 2
OFFS = [sum(n for _, n in RUNS[:i]) for i in range(len(RUNS))]
HH = 4
GROUPS, PER = 5, 25
HID, E = 256, 8
PAIR = 2
PAIR_STEPS = PAIR * NT // 2
EPS = 1e-5
LOWEST = -3.0e38
LR, WD, GEPS = 1e-3, 1e-2, 1e-8
ALR_SCALE = 0.1 * 2.0 / D


class Alone:

    def __init__(self, engine, passed):
        self.engine, self.passed = engine, passed

    def wait_ge(self, semaphore, value):
        self.engine.wait_ge(semaphore, value)
        if not isinstance(value, int):
            self.engine.sem_inc(self.passed, 1)


def tower(nc, xT, w_in, b_in, w_out, b_out, core, taps, w_rope, w_v, pk_q, pk_keys, w_q, kv_table,
          w_o, m_k, m_q, m_v, m_lr, m_blr, m_params, m_b, m_w1T, f_w1, f_b1, f_wg, f_bg, f_wd,
          f_bd, c_rope, c_decay, c_mask, c_ident, c_iota, c_headoff, c_headmask, out):
    with ExitStack() as ctx:
        def sb(name, shape, dt=F32):
            return ctx.enter_context(nc.sbuf_tensor(name, shape, dt))

        def bank(name, n=1):
            return ctx.enter_context(nc.psum_tensor(name, [128, n, 512], F32))

        def sem(name):
            return ctx.enter_context(nc.semaphore(name))

        ident = sb("ident", [128, 128])
        rope_t = sb("rope_t", [D, 2, 2, S])
        decay = sb("decay", [P, S])
        mask = sb("mask", [P, 2, S])
        iota = sb("iota", [P, CAND])
        headoff = sb("headoff", [P, H, K])
        headmask = sb("headmask", [128, H])
        win_s = sb("win_s", [D, 2, D])
        wout_s = sb("wout_s", [D, 2, D])
        bias_s = sb("bias_s", [D, 4])
        core_s = sb("core_s", [D, 2])
        taps_s = sb("taps_s", [D, TAPS])
        tapdiag = sb("tapdiag", [D, TAPS, D])
        wrope_s = sb("wrope_s", [D, 4, D])
        wv_s = sb("wv_s", [D, D])
        simw = sb("simw", [D, 2 * H * SUB])
        wq_s = sb("wq_s", [D, H, D])
        wo_s = sb("wo_s", [128, H, D])
        mk_s = sb("mk_s", [D, D])
        mq_s = sb("mq_s", [D, D])
        mv_s = sb("mv_s", [D, D])
        mlr_s = sb("mlr_s", [D, 1])
        mlrb = sb("mlrb", [D, D])
        mblr_s = sb("mblr_s", [D, 1])
        params = sb("params", [D + 1, 2, D])
        mb_s = sb("mb_s", [D, 2])
        w1T_s = sb("w1T_s", [D, D])
        fw1_s = sb("fw1_s", [D, HID])
        fb1_s = sb("fb1_s", [128, HID // 128])
        fwg_s = sb("fwg_s", [128, HID // 128, E])
        fbg_s = sb("fbg_s", [P, E])
        fwd_s = sb("fwd_s", [128, HID // 128, E * D])
        eps = sb("eps", [P, 1])
        spare = sb("spare", [1, 8])
        h2_saved = nc.dram_tensor("h2_saved", (B, P, NT * D), F32).ap()
        queries_kept = nc.dram_tensor("queries_kept", (B, D, S), F32).ap()
        grads = sb("grads", [D + 1, 2 * D])
        x_in = sb("x_in", [D, S_IN])
        front = sb("front", [128, 4 * HALF])
        tok = front[0:D].rearrange("p (n c t) -> p n c t", n=2, c=2)
        mixed = sb("mixed", [D, S_IN + 2 * PAD])
        h0 = sb("h0", [P, NT, D])
        stats = sb("stats", [P, NT, 6])
        mv = sb("mv", [P, NT, 2])
        std = sb("std", [P, NT])
        rstd = sb("rstd", [P, NT])
        nrm = sb("nrm", [P, NT, D])
        nT = sb("nT", [D, S])
        shared = sb("shared", [128, 4 * S + NT * H * D])
        ret = shared[0:P, 0:NT * S].rearrange("p (j s) -> p j s", j=NT)
        qk = sb("qk", [D, 2, S])
        qk_b = shared[0:D, NT * S:(NT + 2) * S].rearrange("p (j s) -> p j s", j=2)
        v_s = sb("v_s", [P, NT, D])
        h1 = sb("h1", [P, NT, D])
        n2T = sb("n2T", [D, S])
        s16 = sb("s16", [P, 2 * H, K])
        i16 = sb("i16", [P, 2 * H, K], U32)
        i16f = sb("i16f", [P, 2 * H, K])
        rest = front[0:P, 0:2 * H * SUB].rearrange("p (g k) -> p g k", k=SUB)
        cand = sb("cand", [P, H, CAND])
        cidx = sb("cidx", [P, H, CAND])
        crest = front[0:P, 2 * H * SUB:2 * H * SUB + H * CAND].rearrange("p (h c) -> p h c", c=CAND)
        f16 = sb("f16", [P, H, K])
        pos = sb("pos", [P, H, K], U32)
        posf = sb("posf", [P, H, K])
        picks = sb("picks", [128, HH * K * CAND])
        pick = picks[0:P].rearrange("p (n c) -> p n c", c=CAND)
        idxf = sb("idxf", [P, H, K])
        esum = sb("esum", [P, 2, H])
        wgt = sb("wgt", [P, H, K])
        wT_next = sb("wT_next", [128, S])
        idx_next = sb("idx_next", [128, S], U32)
        idx_now = sb("idx_now", [128, S], U32)
        wbd = sb("wbd", [128, S, H])
        rows = sb("rows", [128, GROUPS * PER, 2 * D])
        kvT = sb("kvT", [128, H, S])
        h1_now = sb("h1_now", [P, NT, D])
        n2T_now = sb("n2T_now", [D, S])
        vo = shared[0:P, 4 * S:].rearrange("p (j d) -> p j d", j=NT)
        qT = sb("qT", [D, 2, S])
        prob2 = sb("prob2", [P, 2 * S])
        prob = [shared[0:P, 0:2 * S].rearrange("p (j s) -> p j s", j=2), prob2[:].rearrange("p (j s) -> p j s", j=2)]
        pT = shared[0:P, 2 * S:4 * S].rearrange("p (j s) -> p j s", j=2)
        mx = sb("mx", [P, 2, NT])
        zs = sb("zs", [P, 4, NT])

        def regions(h):
            p = prob[h % 2]
            return p[:, 0, 0:P], p[:, 0, P:S], p[:, 1, 0:S]

        h2 = sb("h2", [P, NT, D])
        x0 = sb("x0", [D + 1, S])
        x1 = sb("x1", [D + 1, S])
        x2 = sb("x2", [D, S])
        sg = picks[0:D, 0:3 * S].rearrange("p (j s) -> p j s", j=3)
        s_a = picks[0:D, 3 * S:5 * S].rearrange("p (j s) -> p j s", j=2)
        d_a = picks[0:D, 5 * S:7 * S].rearrange("p (j s) -> p j s", j=2)
        g2 = picks[0:D, 7 * S:8 * S]
        n3T = sb("n3T", [D, S])
        dz = sb("dz", [D, 2, S])
        xt = sb("xt", [P, 2, NT, D + 1])
        dzt = sb("dzt", [P, 2, NT, D])
        upd = sb("upd", [D + 1, 3, 2 * D])
        lmax = sb("lmax", [P, 3, PAIR * NT])
        e8 = sb("e8", [P, PAIR * NT, E])
        p8 = sb("p8", [P, PAIR * NT, E])
        m8 = sb("m8", [P, PAIR * NT, 8])
        mi8 = sb("mi8", [P, PAIR * NT, 8], U32)
        mif = sb("mif", [P, PAIR * NT])
        c8 = sb("c8", [P, PAIR * NT, E])
        pkq_s = rows[0:D // 2, 0:8, :].rearrange("p a d -> p (a d)").rearrange("p (g d) -> p g d", d=D)
        pkk_s = rows[0:D // 2, 8:16, :].rearrange("p a d -> p (a d)").rearrange("p (g d) -> p g d", d=SUB)

        work = bank("work", 2)
        sims = bank("sims", 2)
        gath = bank("gath", 2)
        turn = bank("turn")
        accu = bank("accu")

        names = """loaded_first loaded fold_mm fold_done prep tapd x_in tok_mm tok_act tok_sq conv h0_done
            ln_stats ln_var ln_std ln_inv ln_n nT_mm nT_done ml_stats ml_var ml_std ml_inv ml_n nTm_mm
            nTm_done qk_mm v_done rope_a rope_b rope_done ret_mm ret_done mix_mm h1_done sim_mm sim_read
            top_a top_b top_c top_d cand_a cand_b fin_a fin_b fin_c fin_d pos_f pick_a pick_b pick_c
            fdiff fexp fsum frec wgt_done tw_mm wT_done next_ready idx_taken wbd_done kept freed kv_done
            vo_mm vo_done q_mm q_done s_mm s_masked s_max s_exp s_rec s_norm pT_mm pT_done o_mm h2_done
            h2_kept queries_sent mq_done x0_mm x0_done alr_done z_mm sig_done silu_a x_done dd_a d_done
            err_a g2_done dz2_done dx_mm g1_done dz_done t_mm t_done g_mm g_done upd_a upd_b upd_c upd_d
            upd_e upd_done out_ready out_sent t_h2 t_x0 t_z t_sig t_silu t_x t_tr t_h3 t_stats t_var
            t_std t_inv t_norm t_turn t_bias t_nT t_res t_ones saved sent h_mm h_act y_mm lg_mm lg_d
            lg_bias y_bias lg_rec lg_max lg_exp lg_sum lg_p lg_top lg_i lg_if lg_oh lg_c wy wy_sum
            pe_waits act_waits dve_waits sp_waits pool_waits""".split()
        assert len(names) == len(set(names))
        s = {n: sem(n) for n in names}
        got = [sem(f"got{g}") for g in range(GROUPS)]

        first_loads = [(win_s, w_in.rearrange("n i o -> i n o")), (bias_s[:, 0:2], b_in),
                       (wout_s, w_out.rearrange("n i o -> i n o")), (bias_s[:, 2:4], b_out),
                       (core_s[:, 0:1], core.rearrange("(d a) -> d a", a=1)), (ident, c_ident),
                       (taps_s, taps.rearrange("(a t) -> a t", a=1).broadcast_to([D, TAPS]))]
        loads = [(pkq_s, pk_q), (pkk_s, pk_keys), (wrope_s, w_rope), (wv_s, w_v), (rope_t, c_rope), (decay, c_decay), (mask, c_mask), (iota, c_iota),
                 (headoff, c_headoff), (headmask, c_headmask),
                 (wq_s, w_q.rearrange("i (h o) -> i h o", h=H)),
                 (wo_s[D:128], w_o.rearrange("(h d) o -> d h o", h=H)),
                 (mk_s, m_k), (mq_s, m_q), (mv_s, m_v), (mlr_s, m_lr),
                 (mblr_s, m_blr.rearrange("(a t) -> a t", a=1).broadcast_to([D, 1])),
                 (params, m_params), (mb_s, m_b), (w1T_s, m_w1T),
                 (fw1_s, f_w1), (fb1_s, f_b1),
                 (fwg_s, f_wg.rearrange("(c p) e -> p c e", p=128)),
                 (fbg_s, f_bg.rearrange("(a t) -> a t", a=1).broadcast_to([P, E])), (fwd_s, f_wd)]
        FIRST_LOADED = 16 * len(first_loads)
        ALL_LOADED = 16 * len(loads)

        def tile(t):
            return slice(t * P, (t + 1) * P)

        flat = rows[:].rearrange("p n d -> p (n d)")
        used = [0]

        def tail(parts, *shape):
            at = used[0]
            used[0] += int(np.prod(shape))
            assert used[0] <= GROUPS * PER * 2 * D
            x = flat[0:parts, at:used[0]]
            if len(shape) == 1:
                return x
            names = "abcd"[:len(shape)]
            return x.rearrange(f"p ({' '.join(names)}) -> p {' '.join(names)}", **dict(zip(names, shape)))

        x0_p = tail(D + 1, PAIR, S)
        x1_p = tail(D + 1, PAIR, S)
        x2_p = tail(D, PAIR, S)
        sg_p = tail(D, PAIR, S)
        silu_p = tail(D, PAIR, S)
        nT_p = tail(D, PAIR, S)
        hid = tail(128, HID // 128, PAIR, S)
        h2_p = tail(P, PAIR * NT * D)
        h3_p = tail(P, PAIR * NT, D)
        nrm_p = tail(P, PAIR * NT, D)
        out_p = tail(P, PAIR * NT, D)
        stats_p = tail(P, PAIR * NT, 6)
        mv_p = tail(P, PAIR * NT, 2)
        std_p = tail(P, PAIR * NT)
        rstd_p = tail(P, PAIR * NT)
        lg = tail(P, PAIR * NT, E)
        fbd_p = tail(P, E * D)
        wy = tail(P, 2, E, D)
        ysum = tail(P, 2, D)
        PAIRS = [(0, 0, 0), (1, 0, P), (1, 1, 2 * P), (2, 0, 0), (2, 1, P), (2, 2, 2 * P)]

        block = ctx.enter_context(nc.Block())

        @block.sync
        def _(sp):
            sp = Alone(nc.sync, s["sp_waits"])

            def load_x(b):
                nc.sync.dma_start(x_in[:], xT[b]).then_inc(s["x_in"], 16)

            def keep(b):
                sp.wait_ge(s["mq_done"], b + 1)
                nc.sync.dma_start(queries_kept[b], n3T[:]).then_inc(s["queries_sent"], 16)
                nc.sync.dma_start(h2_saved[b], h2[:].rearrange("p t d -> p (t d)")).then_inc(s["h2_kept"], 16)
                sp.wait_ge(s["queries_sent"], b * 16 + 16)
                sp.wait_ge(s["h2_kept"], b * 16 + 16)
                nc.sync.sem_inc(s["saved"], 1)

            load_x(0)
            for dst, src in first_loads[0::2]:
                nc.sync.dma_start(dst[:], src).then_inc(s["loaded_first"], 16)
            for dst, src in loads:
                nc.sync.dma_start(dst[:], src).then_inc(s["loaded"], 16)
            nc.sync.sem_inc(s["saved"], 1)
            nc.sync.sem_inc(s["sent"], 1)
            with nc.sync.Fori(0, B - 1) as b:
                sp.wait_ge(s["tok_mm"], b * 4 + 1)
                load_x(b + 1)
                keep(b)
            keep(B - 1)
            def load_saved(p):
                sp.wait_ge(s["t_x"], p * 2 + 1)
                for c in range(PAIR):
                    nc.sync.dma_start(x0_p[0:D, c, :], queries_kept[PAIR * p + c]).then_inc(s["t_x0"], 16)
                sp.wait_ge(s["t_h3"], p + 1)
                for c in range(PAIR):
                    nc.sync.dma_start(h2_p[:, c * NT * D:(c + 1) * NT * D], h2_saved[PAIR * p + c]).then_inc(s["t_h2"], 16)

            def send(p):
                sp.wait_ge(s["out_ready"], p * PAIR_STEPS + PAIR_STEPS)
                for c in range(PAIR):
                    nc.sync.dma_start(out[PAIR * p + c].rearrange("(t p) d -> p t d", p=P),
                                      out_p[:, c * NT:(c + 1) * NT, :]).then_inc(s["out_sent"], 16)
                sp.wait_ge(s["out_sent"], p * (16 * PAIR) + 16 * PAIR)
                nc.sync.sem_inc(s["sent"], 1)

            sp.wait_ge(s["freed"], GROUPS * (B * NT + 1))
            nc.sync.dma_start(fbd_p, f_bd.broadcast_to([P, E * D])).then_inc(s["t_bias"], 16)
            nc.sync.sem_inc(s["t_x"], 2)
            nc.sync.sem_inc(s["t_h3"], 1)
            load_saved(0)
            load_saved(1)
            with nc.sync.Fori(1, B // PAIR - 1) as p:
                load_saved(p + 1)
                send(p - 1)
            send(B // PAIR - 2)
            send(B // PAIR - 1)

        @block.gpsimd
        def _(pool):
            pool = Alone(nc.gpsimd, s["pool_waits"])

            nc.gpsimd.memset(mixed[:], 0.0)
            nc.gpsimd.memset(x0[:], 1.0)
            nc.gpsimd.memset(x1[:], 1.0)
            nc.gpsimd.memset(eps[:], EPS)
            nc.gpsimd.memset(grads[:], 0.0)
            nc.gpsimd.memset(xt[:], 1.0).then_inc(s["prep"], 1)

            with nc.gpsimd.Fori(0, B) as b:
                for t in range(NT):
                    pool.wait_ge(s["next_ready"], b * NT + t + 1)
                    nc.gpsimd.tensor_copy(idx_now[:, tile(t)], idx_next[:, tile(t)]).then_inc(s["idx_taken"], 1)
                    pool.wait_ge(s["idx_taken"], b * NT + t + 1)
                    for g in range(GROUPS):
                        pool.wait_ge(s["freed"], b * (NT * GROUPS) + (t * GROUPS + g + 1))
                        for j in range(PER):
                            n = g * PER + j
                            nc.gpsimd.indirect_dma_start(
                                rows[:, n, :], None, kv_table,
                                bass.IndirectOffsetOnAxis(ap=idx_now[:, t * P + n:t * P + n + 1], axis=0),
                            ).then_inc(got[g], 16)

        @block.tensor
        def _(pe):
            pe = Alone(nc.tensor, s["pe_waits"])

            mm, tr = nc.tensor.matmul, nc.tensor.transpose

            def turned(done):
                for t in range(NT):
                    last = tr(turn[0:D, 0, tile(t)], nrm[:, t, :], ident[0:P, 0:P])
                last.then_inc(done, 1)

            def fold():
                pe.wait_ge(s["loaded"], ALL_LOADED)
                for ph in range(2 * H):
                    last = mm(sims[0:D, ph // H, (ph % H) * SUB:(ph % H + 1) * SUB], pkq_s[:, ph, :], pkk_s[:, ph, :],
                              start=True, stop=True)
                last.then_inc(s["fold_mm"], 1)
                pe.wait_ge(s["fold_done"], 1)

            def prepare(b):
                pe.wait_ge(s["x_in"], b * 16 + 16)
                for n, (w, src) in enumerate([(win_s[:, 0], x_in), (win_s[:, 1], 0), (wout_s[:, 1], 1), (wout_s[:, 0], 0)]):
                    if n == 1:
                        pe.wait_ge(s["tok_act"], b * 4 + 1)
                    if n == 2:
                        pe.wait_ge(s["tok_sq"], b + 1)
                    if n == 3:
                        pe.wait_ge(s["tok_act"], b * 4 + 3)
                    for c in range(2):
                        rhs = x_in[:, c * HALF:(c + 1) * HALF] if n == 0 else tok[:, src, c, :]
                        last = mm(work[0:D, c, 0:HALF], w, rhs, start=True, stop=True)
                    last.then_inc(s["tok_mm"], 1)
                if isinstance(b, int) and b == 0:
                    pe.wait_ge(s["tapd"], 1)
                pe.wait_ge(s["tok_act"], b * 4 + 4)
                for t in range(NT):
                    for k in range(TAPS):
                        at = STRIDE * t * P + k
                        last = mm(work[0:P, 0, t * D:(t + 1) * D], mixed[:, at:at + STRIDE * (P - 1) + 1:STRIDE],
                                  tapdiag[:, k, :], start=(k == 0), stop=(k == TAPS - 1))
                last.then_inc(s["conv"], 1)
                if isinstance(b, int) and b == 0:
                    fold()
                pe.wait_ge(s["ln_n"], b * 2 + 1)
                turned(s["nT_mm"])
                pe.wait_ge(s["nT_done"], b * 2 + 1)
                for c in range(2):
                    mm(work[0:D, c, 0:S], wrope_s[:, c], nT[:], start=True, stop=True)
                    mm(sims[0:D, c, 0:S], wrope_s[:, 2 + c], nT[:], start=True, stop=True)
                for t in range(NT):
                    last = mm(turn[0:P, 0, t * D:(t + 1) * D], nT[:, tile(t)], wv_s[:], start=True, stop=True)
                last.then_inc(s["qk_mm"], 1)
                pe.wait_ge(s["rope_done"], b + 1)
                for j, dst in enumerate((work[0:P, 0], work[0:P, 1], sims[0:P, 0])):
                    last = mm(dst[:, 0:S - j * P], qk[:, 1, tile(j)], qk[:, 0, j * P:S], start=True, stop=True)
                last.then_inc(s["ret_mm"], 1)
                pe.wait_ge(s["ret_done"], b + 1)
                pe.wait_ge(s["v_done"], b + 1)
                for i in range(NT):
                    for j in range(i + 1):
                        last = mm(turn[0:P, 0, i * D:(i + 1) * D], ret[:, j, tile(i - j)], v_s[:, j, :],
                                  start=(j == 0), stop=(j == i))
                last.then_inc(s["mix_mm"], 1)
                pe.wait_ge(s["ln_n"], b * 2 + 2)
                turned(s["nT_mm"])

            def similarities(b, t):
                if t == 0:
                    pe.wait_ge(s["nT_done"], b * 2 + 2)
                else:
                    pe.wait_ge(s["sim_read"], b * NT + t)
                for c in range(2):
                    last = mm(sims[0:P, c, :], n2T[:, tile(t)], simw[:, c * 512:(c + 1) * 512], start=True, stop=True)
                last.then_inc(s["sim_mm"], 1)

            def turn_picks(b, t):
                pe.wait_ge(s["wgt_done"], b * NT + t + 1)
                tr(turn[:, 0, 0:P], wgt[:].rearrange("p h k -> p (h k)"), ident[0:P, 0:P])
                tr(turn[:, 0, P:2 * P], idxf[:].rearrange("p h k -> p (h k)"), ident[0:P, 0:P]).then_inc(s["tw_mm"], 1)

            def take_rows(b, t):
                pe.wait_ge(s["wbd_done"], b * NT + t + 1)
                for g in range(GROUPS):
                    pe.wait_ge(got[g], b * (NT * PER * 16) + (t + 1) * PER * 16)
                    if g == 0:
                        pe.wait_ge(s["kv_done"], b * NT + t + 1)
                    for j in range(PER):
                        n = g * PER + j
                        last = mm(gath[:, n // 64, (n % 64) * H:(n % 64 + 1) * H], rows[:, n, :], wbd[:, t * P + n, :],
                                  start=True, stop=True)
                    last.then_inc(s["freed"], 1)

            def attention(b):
                pe.wait_ge(s["kv_done"], b * NT + NT + 1)
                for j in range(NT):
                    if j >= 1:
                        pe.wait_ge(s["vo_done"], b * NT + j)
                    for h in range(H):
                        last = mm(work[0:P, 0, h * D:(h + 1) * D], kvT[D:128, h, tile(j)], wo_s[D:128, h, :],
                                  start=True, stop=True)
                    last.then_inc(s["vo_mm"], 1)
                pe.wait_ge(s["vo_done"], b * NT + NT)
                def queries(h):
                    mm(work[0:D, 0, 0:S], wq_s[:, h], n2T_now[:], start=True, stop=True).then_inc(s["q_mm"], 1)

                def scores(h):
                    pe.wait_ge(s["q_done"], b * H + h + 1)
                    if h >= 1:
                        pe.wait_ge(s["s_masked"], b * H + h)
                    for i, dst in enumerate((sims[0:P, 0, 0:P], sims[0:P, 0, P:S], sims[0:P, 1, 0:S])):
                        last = mm(dst, qT[:, h % 2, tile(i)], kvT[0:D, h, 0:(i + 1) * P], start=True, stop=True)
                    last.then_inc(s["s_mm"], 1)

                def mix(h):
                    pe.wait_ge(s["pT_done"], b * H + h + 1)
                    for c, (i, j, at) in enumerate(PAIRS):
                        last = mm(accu[0:P, 0, i * D:(i + 1) * D], pT[:, c // 3, at:at + P], vo[:, j, h * D:(h + 1) * D],
                                  start=(h == 0 and c == 0), stop=(h == H - 1 and c == 5), skip_group_check=True)
                    return last

                queries(0)
                scores(0)
                queries(1)
                for h in range(H):
                    if h + 1 < H:
                        scores(h + 1)
                    if h + 2 < H:
                        queries(h + 2)
                    if h >= 1:
                        mix(h - 1)
                    pe.wait_ge(s["s_norm"], b * H + h + 1)
                    for c, (i, j, at) in enumerate(PAIRS):
                        dst = work[0:P, 1, at:at + P] if c < 3 else turn[0:P, 0, at:at + P]
                        last = tr(dst, prob[h % 2][:, c // 3, at:at + P], ident[0:P, 0:P])
                    last.then_inc(s["pT_mm"], 1)
                mix(H - 1).then_inc(s["o_mm"], 1)

            def gradient(b):
                pe.wait_ge(s["ml_n"], b + 1)
                turned(s["nTm_mm"])
                pe.wait_ge(s["nTm_done"], b + 1)
                mm(work[0:D, 0, 0:S], mk_s[:], n3T[:], start=True, stop=True)
                mm(work[0:D, 1, 0:S], mv_s[:], n3T[:], start=True, stop=True)
                mm(turn[0:D, 0, 0:S], mq_s[:], n3T[:], start=True, stop=True)
                mm(sims[0:D, 0, 0:S], mlrb[:], n3T[:], start=True, stop=True).then_inc(s["x0_mm"], 1)
                pe.wait_ge(s["x0_done"], b + 1)
                mm(sims[0:D, 1, 0:S], params[0:D, 0, :], x0[0:D, :], start=True, stop=True).then_inc(s["z_mm"], 1)
                pe.wait_ge(s["x_done"], b * 2 + 1)
                pe.wait_ge(s["mq_done"], b + 1)
                mm(turn[0:D, 0, 0:S], params[0:D, 1, :], x1[0:D, :], start=True, stop=True).then_inc(s["z_mm"], 1)
                pe.wait_ge(s["dz2_done"], b + 1)
                mm(work[0:D, 0, 0:S], w1T_s[:], dz[:, 1, :], start=True, stop=True).then_inc(s["dx_mm"], 1)
                pe.wait_ge(s["dz_done"], b + 1)
                for l in range(2):
                    for t in range(NT):
                        tr(sims[0:P, l, t * D:(t + 1) * D], (x0, x1)[l][0:D, tile(t)], ident[0:D, 0:D])
                        last = tr(sims[0:P, l, 192 + t * D:192 + (t + 1) * D], dz[:, l, tile(t)], ident[0:D, 0:D])
                last.then_inc(s["t_mm"], 1)
                pe.wait_ge(s["t_done"], b + 1)
                for l in range(2):
                    for t in range(NT):
                        last = mm(accu[0:D + 1, 0, 256 + l * D:256 + (l + 1) * D], xt[:, l, t, :], dzt[:, l, t, :],
                                  start=(t == 0), stop=(t == NT - 1))
                last.then_inc(s["g_mm"], 1)

            def retrieve(p, chosen):
                if chosen:
                    pe.wait_ge(s["h_act"], p * 2 - 1)
                pe.wait_ge(s["t_x0"], p * (16 * PAIR) + 16 * PAIR)
                for c in range(PAIR):
                    last = mm(sims[0:D, c, 0:S], upd[:, 2, 0:D], x0_p[:, c, :], start=True, stop=True)
                last.then_inc(s["t_z"], 1)
                if chosen:
                    logits(p - 1)
                pe.wait_ge(s["t_x"], p * 2 + 3)
                for c in range(PAIR):
                    last = mm(sims[0:D, c, 0:S], upd[:, 2, D:2 * D], x1_p[:, c, :], start=True, stop=True)
                last.then_inc(s["t_z"], 1)
                if chosen:
                    experts(p - 1, 0)
                pe.wait_ge(s["t_x"], p * 2 + 4)
                for n in range(PAIR * NT):
                    last = tr(work[0:P, 0, n * D:(n + 1) * D], x2_p[:, n // NT, tile(n % NT)], ident[0:D, 0:D])
                last.then_inc(s["t_tr"], 1)
                if chosen:
                    experts(p - 1, 1)
                    experts(p - 1, 2)
                pe.wait_ge(s["t_norm"], p + 1)
                for n in range(PAIR * NT):
                    last = tr(sims[0:D, n // NT, tile(n % NT)], nrm_p[:, n, :], ident[0:P, 0:P])
                last.then_inc(s["t_turn"], 1)
                pe.wait_ge(s["t_nT"], p + 1)
                for half, dst in ((1, sims), (0, work)):
                    for c in range(PAIR):
                        last = mm(dst[:, c, 0:S], fw1_s[:, half * 128:(half + 1) * 128], nT_p[:, c, :], start=True, stop=True)
                    last.then_inc(s["h_mm"], 1)

            def logits(p):
                pe.wait_ge(s["h_act"], p * 2 + 2)
                for n in range(PAIR * NT):
                    dst = accu[0:P, 0, n * E:(n + 1) * E]
                    for c in range(HID // 128):
                        last = mm(dst, hid[:, c, n // NT, tile(n % NT)], fwg_s[:, c, :], start=(c == 0), stop=(c == HID // 128 - 1))
                last.then_inc(s["lg_mm"], 1)

            def experts(p, k):
                pe.wait_ge(s["y_bias"], p * PAIR_STEPS + (k + 1))
                for n in range(2 * k, 2 * k + 2):
                    dst = gath[0:P, n % 2, :]
                    for c in range(HID // 128):
                        last = mm(dst, hid[:, c, n // NT, tile(n % NT)], fwd_s[:, c, :], start=(c == 0), stop=(c == HID // 128 - 1))
                last.then_inc(s["y_mm"], 1)

            pe.wait_ge(s["loaded_first"], FIRST_LOADED)
            pe.wait_ge(s["prep"], 1)
            nc.tensor.sem_inc(s["freed"], GROUPS)
            nc.tensor.sem_inc(s["kv_done"], 1)
            prepare(0)
            for t in range(2):
                similarities(0, t)
                turn_picks(0, t)
            similarities(0, 2)
            take_rows(0, 0)
            turn_picks(0, 2)
            with nc.tensor.Fori(0, B - 1) as b:
                prepare(b + 1)
                for t in range(2):
                    similarities(b + 1, t)
                    take_rows(b, t + 1)
                    turn_picks(b + 1, t)
                attention(b)
                similarities(b + 1, 2)
                take_rows(b + 1, 0)
                turn_picks(b + 1, 2)
                gradient(b)
            for t in range(1, NT):
                take_rows(B - 1, t)
            attention(B - 1)
            gradient(B - 1)
            nc.tensor.sem_inc(s["y_bias"], 1)
            pe.wait_ge(s["upd_done"], 1)
            retrieve(0, False)
            with nc.tensor.Fori(1, B // PAIR) as p:
                retrieve(p, True)
            logits(B // PAIR - 1)
            for k in range(PAIR_STEPS):
                experts(B // PAIR - 1, k)


        @block.scalar
        def _(act):
            act = Alone(nc.scalar, s["act_waits"])

            fn = nc.scalar.activation

            tables_used = {}

            def table_for(function):
                column = tables_used.setdefault(function, len(tables_used))
                fn(spare[:, column:column + 1], eps[0:1, 0:1], function)

            def deviation(n, var_ready, std_done):
                act.wait_ge(var_ready, n)
                fn(std[:], mv[:, :, 1], ACT.Sqrt, bias=eps[:, 0:1]).then_inc(std_done, 1)

            def keep(b):
                if isinstance(b, int) and b == 0:
                    act.wait_ge(s["nT_done"], 2)
                else:
                    act.wait_ge(s["h2_done"], b)
                nc.scalar.copy(h1_now[:], h1[:])
                nc.scalar.copy(n2T_now[:], n2T[:]).then_inc(s["kept"], 1)

            def prepare(b):
                for n, (dst, bias) in enumerate([(0, 0), (None, 1), (0, 3), (None, 2)]):
                    act.wait_ge(s["tok_mm"], b * 4 + n + 1)
                    if n == 3:
                        to = mixed[:, PAD:PAD + S_IN].rearrange("d (c t) -> d c t", c=2)
                    else:
                        to = tok[:, (0, 1, 0)[n]]
                    fn(to, work[0:D, :, 0:HALF], ACT.Tanh, bias=bias_s[:, bias:bias + 1]).then_inc(s["tok_act"], 1)
                deviation(b * 2 + 1, s["ln_var"], s["ln_std"])
                act.wait_ge(s["nT_mm"], b * 2 + 1)
                nc.scalar.copy(nT[:], turn[0:D, 0, 0:S]).then_inc(s["nT_done"], 1)
                act.wait_ge(s["qk_mm"], b + 1)
                nc.scalar.copy(v_s[:].rearrange("p t d -> p (t d)"), turn[0:P, 0, 0:NT * D]).then_inc(s["v_done"], 1)
                deviation(b * 2 + 2, s["ln_var"], s["ln_std"])
                act.wait_ge(s["nT_mm"], b * 2 + 2)
                nc.scalar.copy(n2T[:], turn[0:D, 0, 0:S]).then_inc(s["nT_done"], 1)

            def soften(b, t):
                act.wait_ge(s["fdiff"], b * NT + t + 1)
                fn(wgt[:], wgt[:], ACT.Exp).then_inc(s["fexp"], 1)

            def turn_weights(b, t):
                act.wait_ge(s["next_ready"], b * NT + t + 1)
                if not (isinstance(b, int) and b == 0):
                    act.wait_ge(s["wbd_done"], b * NT + (t + 1 - NT))
                nc.scalar.copy(wT_next[:, tile(t)], turn[:, 0, 0:P]).then_inc(s["wT_done"], 1)

            def take_rows(b, t):
                act.wait_ge(s["freed"], b * (NT * GROUPS) + (t * GROUPS + 2 * GROUPS))
                nc.scalar.copy(kvT[:, :, t * P:t * P + 64], gath[:, 0, :].rearrange("p (n h) -> p h n", h=H))
                nc.scalar.copy(kvT[:, :, t * P + 64:(t + 1) * P],
                               gath[:, 1, 0:(P - 64) * H].rearrange("p (n h) -> p h n", h=H)).then_inc(s["kv_done"], 1)

            def attention(b):
                for j in range(NT):
                    act.wait_ge(s["vo_mm"], b * NT + j + 1)
                    nc.scalar.copy(vo[:, j, :], work[0:P, 0, :]).then_inc(s["vo_done"], 1)
                def scale_q(h):
                    act.wait_ge(s["q_mm"], b * H + h + 1)
                    nc.scalar.mul(qT[:, h % 2], work[0:D, 0, 0:S], float(D) ** -0.5).then_inc(s["q_done"], 1)

                def exponentials(h):
                    act.wait_ge(s["s_max"], b * H + h + 1)
                    for i, p in enumerate(regions(h)):
                        last = fn(p, p, ACT.Exp, bias=mx[:, h % 2, i:i + 1], accum_out=zs[:, h % 2, i:i + 1])
                    last.then_inc(s["s_exp"], 1)

                scale_q(0)
                scale_q(1)
                exponentials(0)
                for h in range(H):
                    if h + 2 < H:
                        scale_q(h + 2)
                    if h + 1 < H:
                        exponentials(h + 1)
                    act.wait_ge(s["pT_mm"], b * H + h + 1)
                    nc.scalar.copy(pT[:, 0, :], work[0:P, 1, 0:S])
                    nc.scalar.copy(pT[:, 1, :], turn[0:P, 0, 0:S]).then_inc(s["pT_done"], 1)

            def gradient(b):
                deviation(b + 1, s["ml_var"], s["ml_std"])
                act.wait_ge(s["nTm_mm"], b + 1)
                act.wait_ge(s["saved"], b + 1)
                nc.scalar.copy(n3T[:], turn[0:D, 0, 0:S]).then_inc(s["nTm_done"], 1)
                act.wait_ge(s["x0_mm"], b + 1)
                nc.scalar.copy(x0[0:D, :], work[0:D, 0, 0:S]).then_inc(s["x0_done"], 1)
                fn(sg[:, 2, :], sims[0:D, 0, 0:S], ACT.Sigmoid, bias=mblr_s[:, 0:1]).then_inc(s["alr_done"], 1)
                nc.scalar.copy(n3T[:], turn[0:D, 0, 0:S]).then_inc(s["mq_done"], 1)
                for l, z in enumerate((sims[0:D, 1, 0:S], turn[0:D, 0, 0:S])):
                    act.wait_ge(s["z_mm"], b * 2 + l + 1)
                    fn(sg[:, l, :], z, ACT.Sigmoid, bias=mb_s[:, l:l + 1]).then_inc(s["sig_done"], 1)
                act.wait_ge(s["t_mm"], b + 1)
                for l in range(2):
                    nc.scalar.copy(xt[:, l, :, 0:D], sims[0:P, l, 0:192].rearrange("p (t d) -> p t d", d=D))
                    last = nc.scalar.copy(dzt[:, l, :, :], sims[0:P, l, 192:384].rearrange("p (t d) -> p t d", d=D))
                last.then_inc(s["t_done"], 1)

            def retrieve(p, chosen):
                for l in range(2):
                    act.wait_ge(s["t_z"], p * 2 + (l + 1))
                    fn(sg_p, sims[0:D, :, 0:S], ACT.Sigmoid).then_inc(s["t_sig"], 1)
                    if chosen and l == 0:
                        exp_logits(p - 1)
                        table_for(ACT.Sigmoid)
                table_for(ACT.Sqrt)
                act.wait_ge(s["t_var"], p + 1)
                fn(std_p, mv_p[:, :, 1], ACT.Sqrt, bias=eps[:, 0:1]).then_inc(s["t_std"], 1)
                act.wait_ge(s["t_turn"], p + 1)
                nc.scalar.copy(nT_p, sims[0:D, :, 0:S]).then_inc(s["t_nT"], 1)
                table_for(ACT.Gelu)
                for n, (half, src) in enumerate(((1, sims), (0, work))):
                    act.wait_ge(s["h_mm"], p * 2 + (n + 1))
                    fn(hid[:, half], src[:, :, 0:S], ACT.Gelu, bias=fb1_s[:, half:half + 1]).then_inc(s["h_act"], 1)
                table_for(ACT.Sigmoid)

            def exp_logits(p):
                table_for(ACT.Exp)
                act.wait_ge(s["lg_d"], p + 1)
                fn(e8[:], e8[:], ACT.Exp).then_inc(s["lg_exp"], 1)

            for dst, src in first_loads[1::2]:
                nc.scalar.dma_start(dst[:], src).then_inc(s["loaded_first"], 16)
            act.wait_ge(s["prep"], 1)
            table_for(ACT.Tanh)
            act.wait_ge(s["loaded_first"], FIRST_LOADED)
            prepare(0)
            act.wait_ge(s["loaded"], ALL_LOADED)
            for t in range(2):
                soften(0, t)
                turn_weights(0, t)
            keep(0)
            soften(0, 2)
            take_rows(0, 0)
            turn_weights(0, 2)
            with nc.scalar.Fori(0, B - 1) as b:
                prepare(b + 1)
                for t in range(2):
                    soften(b + 1, t)
                    take_rows(b, t + 1)
                    turn_weights(b + 1, t)
                attention(b)
                keep(b + 1)
                soften(b + 1, 2)
                take_rows(b + 1, 0)
                turn_weights(b + 1, 2)
                gradient(b)
            for t in range(1, NT):
                take_rows(B - 1, t)
            attention(B - 1)
            gradient(B - 1)
            retrieve(0, False)
            with nc.scalar.Fori(1, B // PAIR) as p:
                retrieve(p, True)
            exp_logits(B // PAIR - 1)

        @block.vector
        def _(dve):
            dve = Alone(nc.vector, s["dve_waits"])

            v = nc.vector

            def normalise(src, n, gone, aggregated, deviated, inverted, normalised):
                for t in range(NT):
                    last = v.bn_stats(stats[:, t, :], src[:, t, :])
                last.then_inc(gone, 1)
                dve.wait_ge(gone, n)
                for t in range(NT):
                    last = v.bn_aggr(mv[:, t, :], stats[:, t, :])
                last.then_inc(aggregated, 1)
                dve.wait_ge(deviated, n)
                v.reciprocal(rstd[:], std[:]).then_inc(inverted, 1)
                dve.wait_ge(inverted, n)
                for t in range(NT):
                    last = v.tensor_scalar(nrm[:, t, :], src[:, t, :], mv[:, t, 0:1], rstd[:, t:t + 1],
                                           ALU.subtract, ALU.mult)
                last.then_inc(normalised, 1)

            def prepare(b):
                dve.wait_ge(s["tok_act"], b * 4 + 2)
                for c in range(2):
                    last = v.scalar_tensor_tensor(tok[:, 1, c, :], tok[:, 1, c, :], core_s[:, 0:1], tok[:, 1, c, :],
                                                  ALU.mult, ALU.mult)
                last.then_inc(s["tok_sq"], 1)
                dve.wait_ge(s["conv"], b + 1)
                v.tensor_copy(h0[:].rearrange("p t d -> p (t d)"), work[0:P, 0, 0:NT * D]).then_inc(s["h0_done"], 1)
                dve.wait_ge(s["h0_done"], b + 1)
                normalise(h0, b * 2 + 1, s["ln_stats"], s["ln_var"], s["ln_std"], s["ln_inv"], s["ln_n"])
                if isinstance(b, int) and b == 0:
                    dve.wait_ge(s["loaded"], ALL_LOADED)
                    v.tensor_copy(mlrb[:], mlr_s[:].broadcast_to([D, D]))
                    dve.wait_ge(s["fold_mm"], 1)
                    v.tensor_copy(simw[:], sims[0:D].rearrange("p c k -> p (c k)")).then_inc(s["fold_done"], 1)
                dve.wait_ge(s["qk_mm"], b + 1)
                v.tensor_tensor(qk[:], work[0:D, :, 0:S], rope_t[:, 0], ALU.mult).then_inc(s["rope_a"], 1)
                v.tensor_tensor(qk_b, sims[0:D, :, 0:S], rope_t[:, 1], ALU.mult).then_inc(s["rope_b"], 1)
                dve.wait_ge(s["rope_a"], b + 1)
                dve.wait_ge(s["rope_b"], b + 1)
                v.tensor_tensor(qk[:], qk[:], qk_b, ALU.add).then_inc(s["rope_done"], 1)
                dve.wait_ge(s["ret_mm"], b + 1)
                for j, src in enumerate((work[0:P, 0], work[0:P, 1], sims[0:P, 0])):
                    last = v.tensor_tensor(ret[:, j, 0:S - j * P], src[:, 0:S - j * P], decay[:, 0:S - j * P], ALU.mult)
                last.then_inc(s["ret_done"], 1)
                dve.wait_ge(s["mix_mm"], b + 1)
                if not (isinstance(b, int) and b == 0):
                    dve.wait_ge(s["kept"], b)
                v.tensor_tensor(h1[:].rearrange("p t d -> p (t d)"), h0[:].rearrange("p t d -> p (t d)"),
                                turn[0:P, 0, 0:NT * D], ALU.add).then_inc(s["h1_done"], 1)
                dve.wait_ge(s["h1_done"], b + 1)
                normalise(h1, b * 2 + 2, s["ln_stats"], s["ln_var"], s["ln_std"], s["ln_inv"], s["ln_n"])

            def pick_rows(b, t):
                n = b * NT + t + 1
                dve.wait_ge(s["sim_mm"], n)
                sim = sims[0:P].rearrange("p c (g k) -> p (c g) k", k=SUB)
                for g in range(2 * H):
                    last = v.max(s16[:, g, 0:8], sim[:, g, :])
                last.then_inc(s["top_a"], 1)
                dve.wait_ge(s["top_a"], n)
                for g in range(2 * H):
                    v.max_index(i16[:, g, 0:8], s16[:, g, 0:8], sim[:, g, :])
                    last = v.match_replace(rest[:, g, :], s16[:, g, 0:8], sim[:, g, :], LOWEST)
                last.then_inc(s["sim_read"], 1)
                dve.wait_ge(s["sim_read"], n)
                for g in range(2 * H):
                    last = v.max(s16[:, g, 8:16], rest[:, g, :])
                last.then_inc(s["top_b"], 1)
                dve.wait_ge(s["top_b"], n)
                for g in range(2 * H):
                    last = v.max_index(i16[:, g, 8:16], s16[:, g, 8:16], rest[:, g, :])
                last.then_inc(s["top_c"], 1)
                dve.wait_ge(s["top_c"], n)
                v.tensor_copy(i16f[:, 0:H], i16[:, 0:H])
                v.scalar_tensor_tensor(i16f[:, H:], i16[:, H:], float(SUB), headoff[:], ALU.mult,
                                       ALU.add).then_inc(s["top_d"], 1)
                dve.wait_ge(s["top_d"], n)
                for src, dst, signal in ((s16, cand, s["cand_a"]), (i16f, cidx, s["cand_b"])):
                    for (a, m), off in zip(RUNS, OFFS):
                        v.tensor_tensor(dst[:, :, off:off + m], src[:, H:, 0:m],
                                        src[:, 0:H, a:a + 1].broadcast_to([P, H, m]), ALU.add)
                    v.tensor_tensor(dst[:, :, TAIL_AT:], src[:, 0:H, K // 2:K],
                                    src[:, H:, 0:1].broadcast_to([P, H, K // 2]), ALU.add).then_inc(signal, 1)
                dve.wait_ge(s["cand_a"], n)
                for h in range(H):
                    last = v.max(f16[:, h, 0:8], cand[:, h, :])
                last.then_inc(s["fin_a"], 1)
                dve.wait_ge(s["fin_a"], n)
                for h in range(H):
                    v.max_index(pos[:, h, 0:8], f16[:, h, 0:8], cand[:, h, :])
                    last = v.match_replace(crest[:, h, :], f16[:, h, 0:8], cand[:, h, :], LOWEST)
                last.then_inc(s["fin_b"], 1)
                dve.wait_ge(s["fin_b"], n)
                for h in range(H):
                    last = v.max(f16[:, h, 8:16], crest[:, h, :])
                last.then_inc(s["fin_c"], 1)
                dve.wait_ge(s["fin_c"], n)
                v.tensor_tensor(wgt[:], f16[:], f16[:, :, 0:1].broadcast_to([P, H, K]),
                                ALU.subtract).then_inc(s["fdiff"], 1)
                for h in range(H):
                    last = v.max_index(pos[:, h, 8:16], f16[:, h, 8:16], crest[:, h, :])
                last.then_inc(s["fin_d"], 1)
                dve.wait_ge(s["fin_d"], n)
                v.tensor_copy(posf[:], pos[:]).then_inc(s["pos_f"], 1)
                dve.wait_ge(s["pos_f"], n)
                dve.wait_ge(s["cand_b"], n)
                for c in range(H // HH):
                    at = slice(c * HH, (c + 1) * HH)
                    m = b * (NT * (H // HH)) + (t * (H // HH) + c + 1)
                    v.tensor_tensor(pick,
                                    posf[:, at].rearrange("p h k -> p (h k)").unsqueeze(2).broadcast_to([P, HH * K, CAND]),
                                    iota[:].unsqueeze(1).broadcast_to([P, HH * K, CAND]),
                                    ALU.is_equal).then_inc(s["pick_a"], 1)
                    dve.wait_ge(s["pick_a"], m)
                    four = pick.rearrange("p (h k) c -> p h k c", k=K)
                    v.tensor_tensor(four, four, cidx[:, at].unsqueeze(2).broadcast_to([P, HH, K, CAND]),
                                    ALU.mult).then_inc(s["pick_b"], 1)
                    dve.wait_ge(s["pick_b"], m)
                    v.tensor_reduce(idxf[:, at].rearrange("p h k -> p (h k)"), pick, AX_X,
                                    ALU.add).then_inc(s["pick_c"], 1)
                    dve.wait_ge(s["pick_c"], m)
                dve.wait_ge(s["fexp"], n)
                v.tensor_reduce(esum[:, 0, :], wgt[:], AX_X, ALU.add).then_inc(s["fsum"], 1)
                dve.wait_ge(s["fsum"], n)
                v.reciprocal(esum[:, 1, :], esum[:, 0, :]).then_inc(s["frec"], 1)
                dve.wait_ge(s["frec"], n)
                v.tensor_tensor(wgt[:], wgt[:], esum[:, 1, :].unsqueeze(2).broadcast_to([P, H, K]),
                                ALU.mult).then_inc(s["wgt_done"], 1)
                dve.wait_ge(s["tw_mm"], n)
                if not (isinstance(b, int) and b == 0):
                    dve.wait_ge(s["idx_taken"], b * NT + (t + 1 - NT))
                v.tensor_copy(idx_next[:, tile(t)], turn[:, 0, P:2 * P]).then_inc(s["next_ready"], 1)

            def spread_weights(b, t):
                dve.wait_ge(s["wT_done"], b * NT + t + 1)
                v.tensor_tensor(wbd[:, tile(t)], wT_next[:, tile(t)].unsqueeze(2).broadcast_to([128, P, H]),
                                headmask[:].unsqueeze(1).broadcast_to([128, P, H]), ALU.mult).then_inc(s["wbd_done"], 1)

            def attention(b):
                def softmax_max(h):
                    n = b * H + h + 1
                    dve.wait_ge(s["s_mm"], n)
                    v.tensor_tensor(prob[h % 2], sims[0:P, :, 0:S], mask[:], ALU.add).then_inc(s["s_masked"], 1)
                    dve.wait_ge(s["s_masked"], n)
                    for i, p in enumerate(regions(h)):
                        last = v.tensor_reduce(mx[:, h % 2, i:i + 1], p, AX_X, ALU.max, negate=True)
                    last.then_inc(s["s_max"], 1)

                softmax_max(0)
                for h in range(H):
                    n = b * H + h + 1
                    dve.wait_ge(s["s_exp"], n)
                    v.reciprocal(zs[:, 2 + h % 2, 0:NT], zs[:, h % 2, 0:NT]).then_inc(s["s_rec"], 1)
                    dve.wait_ge(s["s_rec"], n)
                    for i, p in enumerate(regions(h)):
                        last = v.tensor_scalar(p, p, zs[:, 2 + h % 2, i:i + 1], None, ALU.mult)
                    last.then_inc(s["s_norm"], 1)
                    if h + 1 < H:
                        softmax_max(h + 1)
                dve.wait_ge(s["o_mm"], b + 1)
                if not (isinstance(b, int) and b == 0):
                    dve.wait_ge(s["saved"], b + 1)
                v.tensor_tensor(h2[:].rearrange("p t d -> p (t d)"), h1_now[:].rearrange("p t d -> p (t d)"),
                                accu[0:P, 0, 0:NT * D], ALU.add).then_inc(s["h2_done"], 1)
                dve.wait_ge(s["h2_done"], b + 1)

            def gradient(b):
                normalise(h2, b + 1, s["ml_stats"], s["ml_var"], s["ml_std"], s["ml_inv"], s["ml_n"])
                for l, (z, xin, xout) in enumerate(((sims[0:D, 1, 0:S], x0[0:D], x1[0:D]), (turn[0:D, 0, 0:S], x1[0:D], x2[:]))):
                    n = b * 2 + l + 1
                    dve.wait_ge(s["sig_done"], n)
                    if l == 0:
                        dve.wait_ge(s["x0_done"], b + 1)
                    v.scalar_tensor_tensor(s_a[:, l, :], z, mb_s[:, l:l + 1], sg[:, l, :], ALU.add,
                                           ALU.mult).then_inc(s["silu_a"], 1)
                    dve.wait_ge(s["silu_a"], n)
                    v.tensor_tensor(xout, xin, s_a[:, l, :], ALU.add).then_inc(s["x_done"], 1)
                    v.scalar_tensor_tensor(d_a[:, l, :], s_a[:, l, :], 1.0, sg[:, l, :], ALU.subtract,
                                           ALU.mult).then_inc(s["dd_a"], 1)
                    dve.wait_ge(s["dd_a"], n)
                    v.tensor_tensor(d_a[:, l, :], s_a[:, l, :], d_a[:, l, :], ALU.subtract).then_inc(s["d_done"], 1)
                dve.wait_ge(s["x_done"], b * 2 + 2)
                v.tensor_tensor(x2[:], x2[:], work[0:D, 1, 0:S], ALU.subtract).then_inc(s["err_a"], 1)
                dve.wait_ge(s["err_a"], b + 1)
                dve.wait_ge(s["alr_done"], b + 1)
                v.scalar_tensor_tensor(g2, x2[:], ALR_SCALE, sg[:, 2, :], ALU.mult, ALU.mult).then_inc(s["g2_done"], 1)
                dve.wait_ge(s["g2_done"], b + 1)
                dve.wait_ge(s["d_done"], b * 2 + 2)
                v.tensor_tensor(dz[:, 1, :], g2, d_a[:, 1, :], ALU.mult).then_inc(s["dz2_done"], 1)
                dve.wait_ge(s["dx_mm"], b + 1)
                v.tensor_tensor(g2, g2, work[0:D, 0, 0:S], ALU.add).then_inc(s["g1_done"], 1)
                dve.wait_ge(s["g1_done"], b + 1)
                v.tensor_tensor(dz[:, 0, :], g2, d_a[:, 0, :], ALU.mult).then_inc(s["dz_done"], 1)
                dve.wait_ge(s["g_mm"], b + 1)
                v.tensor_tensor(grads[:], grads[:], accu[0:D + 1, 0, 256:256 + 2 * D], ALU.add).then_inc(s["g_done"], 1)

            def retrieve(p, chosen):
                for l, (xin, xout) in enumerate(((x0_p[0:D], x1_p[0:D]), (x1_p[0:D], x2_p))):
                    n = p * 2 + (l + 1)
                    dve.wait_ge(s["t_sig"], n)
                    v.tensor_tensor(silu_p, sims[0:D, :, 0:S], sg_p, ALU.mult).then_inc(s["t_silu"], 1)
                    dve.wait_ge(s["t_silu"], n)
                    v.tensor_tensor(xout, xin, silu_p, ALU.add).then_inc(s["t_x"], 1)
                    if chosen and l == 0:
                        exponents(p - 1)
                    dve.wait_ge(s["t_x"], n + 2)
                if chosen:
                    choose(p - 1)
                    apply_choice(p - 1, 0)
                dve.wait_ge(s["t_tr"], p + 1)
                dve.wait_ge(s["t_h2"], p * (16 * PAIR) + 16 * PAIR)
                v.tensor_tensor(h3_p.rearrange("p t d -> p (t d)"), h2_p, work[0:P, 0, 0:PAIR * NT * D],
                                ALU.add).then_inc(s["t_h3"], 1)
                dve.wait_ge(s["t_h3"], p + 2)
                for n in range(PAIR * NT):
                    last = v.bn_stats(stats_p[:, n, :], h3_p[:, n, :])
                last.then_inc(s["t_stats"], 1)
                dve.wait_ge(s["t_stats"], p + 1)
                for n in range(PAIR * NT):
                    last = v.bn_aggr(mv_p[:, n, :], stats_p[:, n, :])
                last.then_inc(s["t_var"], 1)
                if chosen:
                    apply_choice(p - 1, 1)
                dve.wait_ge(s["t_std"], p + 1)
                v.reciprocal(rstd_p, std_p).then_inc(s["t_inv"], 1)
                dve.wait_ge(s["t_inv"], p + 1)
                for n in range(PAIR * NT):
                    last = v.tensor_scalar(nrm_p[:, n, :], h3_p[:, n, :], mv_p[:, n, 0:1], rstd_p[:, n:n + 1],
                                           ALU.subtract, ALU.mult)
                last.then_inc(s["t_norm"], 1)
                if chosen:
                    apply_choice(p - 1, 2)

            def exponents(p):
                n = p + 1
                dve.wait_ge(s["sent"], p + 1)
                v.tensor_copy(out_p, h3_p).then_inc(s["t_res"], 1)
                dve.wait_ge(s["lg_mm"], n)
                v.tensor_tensor(lg, accu[0:P, 0, 0:PAIR * NT * E].rearrange("p (t e) -> p t e", e=E),
                                fbg_s[:].unsqueeze(1).broadcast_to([P, PAIR * NT, E]), ALU.add).then_inc(s["lg_bias"], 1)
                dve.wait_ge(s["lg_bias"], n)
                v.tensor_reduce(lmax[:, 0, :], lg, AX_X, ALU.max).then_inc(s["lg_max"], 1)
                dve.wait_ge(s["lg_max"], n)
                v.tensor_tensor(e8[:], lg, lmax[:, 0, :].unsqueeze(2).broadcast_to([P, PAIR * NT, E]),
                                ALU.subtract).then_inc(s["lg_d"], 1)

            def choose(p):
                n = p + 1
                dve.wait_ge(s["lg_exp"], n)
                v.tensor_reduce(lmax[:, 1, :], e8[:], AX_X, ALU.add).then_inc(s["lg_sum"], 1)
                dve.wait_ge(s["lg_sum"], n)
                v.reciprocal(lmax[:, 2, :], lmax[:, 1, :]).then_inc(s["lg_rec"], 1)
                dve.wait_ge(s["lg_rec"], n)
                v.tensor_tensor(p8[:], e8[:], lmax[:, 2, :].unsqueeze(2).broadcast_to([P, PAIR * NT, E]),
                                ALU.mult).then_inc(s["lg_p"], 1)
                dve.wait_ge(s["lg_p"], n)
                for t in range(PAIR * NT):
                    last = v.max(m8[:, t, :], p8[:, t, :])
                last.then_inc(s["lg_top"], 1)
                dve.wait_ge(s["lg_top"], n)
                for t in range(PAIR * NT):
                    last = v.max_index(mi8[:, t, :], m8[:, t, :], p8[:, t, :])
                last.then_inc(s["lg_i"], 1)
                dve.wait_ge(s["lg_i"], n)
                v.tensor_copy(mif[:], mi8[:, :, 0]).then_inc(s["lg_if"], 1)
                dve.wait_ge(s["lg_if"], n)
                v.tensor_tensor(c8[:], iota[:, 0:E].unsqueeze(1).broadcast_to([P, PAIR * NT, E]),
                                mif[:].unsqueeze(2).broadcast_to([P, PAIR * NT, E]), ALU.is_equal).then_inc(s["lg_oh"], 1)
                dve.wait_ge(s["lg_oh"], n)
                v.tensor_tensor(c8[:], c8[:], p8[:], ALU.mult).then_inc(s["lg_c"], 1)
                dve.wait_ge(s["lg_c"], n)
                dve.wait_ge(s["t_res"], n)

            def apply_choice(p, k):
                n = p * PAIR_STEPS + k + 1
                two = slice(2 * k, 2 * k + 2)
                dve.wait_ge(s["y_mm"], n)
                v.tensor_tensor(wy, gath[0:P].rearrange("p t (e d) -> p t e d", e=E),
                                fbd_p.rearrange("p (e d) -> p e d", e=E).unsqueeze(1).broadcast_to([P, 2, E, D]),
                                ALU.add).then_inc(s["y_bias"], 1)
                dve.wait_ge(s["y_bias"], n + 1)
                v.tensor_tensor(wy, wy, c8[:, two, :].unsqueeze(3).broadcast_to([P, 2, E, D]), ALU.mult).then_inc(s["wy"], 1)
                dve.wait_ge(s["wy"], n)
                v.tensor_reduce(ysum, wy.rearrange("p t e d -> p t d e"), AX_X, ALU.add).then_inc(s["wy_sum"], 1)
                dve.wait_ge(s["wy_sum"], n)
                v.tensor_tensor(out_p[:, two, :], out_p[:, two, :], ysum, ALU.add).then_inc(s["out_ready"], 1)

            dve.wait_ge(s["loaded_first"], FIRST_LOADED)
            dve.wait_ge(s["prep"], 1)
            v.tensor_scalar(core_s[:, 1:2], core_s[:, 0:1], -1.0, None, ALU.mult).then_inc(s["upd_a"], 1)
            dve.wait_ge(s["upd_a"], 1)
            v.tensor_tensor(core_s[:, 0:1], core_s[:, 0:1], core_s[:, 1:2], ALU.max)
            for k in range(TAPS):
                last = v.tensor_scalar(tapdiag[:, k, :], ident[0:D, 0:D], taps_s[:, k:k + 1], None, ALU.mult)
            last.then_inc(s["tapd"], 1)
            dve.wait_ge(s["tapd"], 1)
            prepare(0)
            for t in range(2):
                pick_rows(0, t)
                spread_weights(0, t)
            pick_rows(0, 2)
            spread_weights(0, 2)
            with nc.vector.Fori(0, B - 1) as b:
                prepare(b + 1)
                for t in range(2):
                    pick_rows(b + 1, t)
                attention(b)
                for t in range(2):
                    spread_weights(b + 1, t)
                pick_rows(b + 1, 2)
                spread_weights(b + 1, 2)
                gradient(b)
            attention(B - 1)
            gradient(B - 1)
            v.memset(x0_p[D:D + 1], 1.0)
            v.memset(x1_p[D:D + 1], 1.0).then_inc(s["t_ones"], 1)
            dve.wait_ge(s["t_ones"], 1)
            dve.wait_ge(s["g_done"], B)
            v.tensor_scalar(upd[:, 0, :], grads[:], -1.0, None, ALU.mult).then_inc(s["upd_b"], 1)
            dve.wait_ge(s["upd_b"], 1)
            v.tensor_tensor(upd[:, 0, :], upd[:, 0, :], grads[:], ALU.max).then_inc(s["upd_b"], 1)
            dve.wait_ge(s["upd_b"], 2)
            v.tensor_scalar(upd[:, 0, :], upd[:, 0, :], GEPS, None, ALU.add).then_inc(s["upd_c"], 1)
            dve.wait_ge(s["upd_c"], 1)
            v.reciprocal(upd[:, 1, :], upd[:, 0, :]).then_inc(s["upd_d"], 1)
            dve.wait_ge(s["upd_d"], 1)
            v.scalar_tensor_tensor(upd[:, 1, :], upd[:, 1, :], LR, grads[:], ALU.mult, ALU.mult).then_inc(s["upd_e"], 1)
            dve.wait_ge(s["upd_e"], 1)
            v.scalar_tensor_tensor(upd[:, 2, :], params[:].rearrange("p l d -> p (l d)"), 1.0 - LR * WD, upd[:, 1, :],
                                   ALU.mult, ALU.subtract).then_inc(s["upd_done"], 1)
            dve.wait_ge(s["t_bias"], 16)
            retrieve(0, False)
            with nc.vector.Fori(1, B // PAIR) as p:
                retrieve(p, True)
            exponents(B // PAIR - 1)
            choose(B // PAIR - 1)
            for k in range(PAIR_STEPS):
                apply_choice(B // PAIR - 1, k)


def tables():
    f = np.float32
    inv = f(1.0) / f(10000.0) ** (np.arange(0, D, 2, dtype=f) / f(D))
    pos = np.arange(S, dtype=f)
    ang = (pos[:, None] * inv[None, :]).astype(f)
    base = (np.arange(0, D, 2, dtype=f) + f(0.4 * D)) / f(1.4 * D)
    scale = base[None, :] ** (pos[:, None] / f(512.0))
    rope = np.zeros((D, 2, 2, S), f)
    for n, by in enumerate((scale, f(1.0) / scale)):
        c, sn = (np.cos(ang) * by).T, (np.sin(ang) * by).T
        rope[:, 0, n] = np.concatenate([c, c])
        rope[:, 1, n] = np.concatenate([-sn, sn])
    ahead = np.arange(S)[None, :] - np.arange(P)[:, None]
    decay = np.where(ahead >= 0, f(0.96875) ** np.maximum(ahead, 0).astype(f), f(0)).astype(f)
    hidden = np.where(np.arange(P)[None, :] > np.arange(P)[:, None], f(LOWEST), f(0))
    mask = np.zeros((P, 2, S), f)
    mask[:, 0, 0:P] = hidden
    mask[:, 0, 2 * P:] = hidden
    mask[:, 1, 2 * P:] = hidden
    iota = np.tile(np.arange(CAND, dtype=f), (P, 1))
    headoff = np.tile((np.arange(H, dtype=f) * NKV)[None, :, None], (P, 1, K))
    headmask = (np.arange(128)[:, None] // K == np.arange(H)[None, :]).astype(f)
    return [rope, decay, mask, np.eye(128, dtype=f), iota, headoff, headmask]


def kernel(**inputs):
    import concourse.bacc as bacc
    from concourse.bass_utils import run_bass_kernel_spmd as run

    a = {k: np.ascontiguousarray(v) for k, v in inputs.items()}
    wq, wk = a["L0_attn_W_Q"], a["L0_attn_W_K"]
    even_odd = lambda w: np.concatenate([w[:, 0::2], w[:, 1::2]], 1)
    odd_even = lambda w: np.concatenate([w[:, 1::2], w[:, 0::2]], 1)
    feeds = [
        a["x"].transpose(0, 2, 1),
        a["L0_tok_W_in"], a["L0_tok_b_in"].T, a["L0_tok_W_out"], a["L0_tok_b_out"].T, a["L0_tok_core_diag"],
        a["L0_tok_conv_filter"],
        np.stack([even_odd(wq), even_odd(wk), odd_even(wq), odd_even(wk)], 1), a["L0_attn_W_V"],
        a["L0_ffn_Wq_pk"].reshape(D, 2 * H, D // 2).transpose(2, 1, 0),
        a["L0_ffn_pk_keys"].transpose(3, 0, 2, 1).reshape(D // 2, 2 * H, SUB),
        a["L0_ffn_Wq"], np.concatenate([a["L0_ffn_keys_table"], a["L0_ffn_values_table"]], 1), a["L0_ffn_Wo"],
        a["L1_attn_Wk"], a["L1_attn_Wq"], a["L1_attn_Wv"], a["L1_attn_Wlr"], a["L1_attn_blr"],
        np.concatenate([a["L1_attn_Ws"], a["L1_attn_bs"][:, None, :]], 1).transpose(1, 0, 2), a["L1_attn_bs"].T,
        a["L1_attn_Ws"][1].T,
        a["L1_ffn_W1"], a["L1_ffn_b1"].reshape(HID // 128, 128).T, a["L1_ffn_Wg"], a["L1_ffn_bg"],
        a["L1_ffn_Wd"].reshape(E, HID // 128, 128, D).transpose(2, 1, 0, 3).reshape(128, HID // 128, E * D),
        a["L1_ffn_bd"].reshape(1, E * D),
    ] + tables()
    nc = bacc.Bacc("TRN2", target_bir_lowering=False, num_devices=1)
    arrays, args = {}, []
    for n, x in enumerate(feeds):
        arrays[f"in_{n}"] = np.ascontiguousarray(x)
        args.append(nc.dram_tensor(f"in_{n}", x.shape, F32, kind="ExternalInput").ap())
    args.append(nc.dram_tensor("out", (B, S, D), F32, kind="ExternalOutput").ap())
    tower(nc, *args)
    return run(nc, [arrays], core_ids=[0]).results[0]["out"]
```
